# Optimizing a Trainium2 kernel written in Bass

```python
import numpy as np
import jax
import jax.numpy as jnp

def _softmax(x, axis=-1):
    return jax.nn.softmax(x, axis=axis)
def _gelu(x):
    return jax.nn.gelu(x, approximate=True)
def _silu(x):
    return jax.nn.silu(x)
def _sigmoid(x):
    return jax.nn.sigmoid(x)
def _layernorm(x, axis=-1, eps=1e-5):
    m = jnp.mean(x, axis=axis, keepdims=True)
    v = jnp.var(x, axis=axis, keepdims=True)
    return (x - m) / jnp.sqrt(v + eps)
def _scatter_add(tgt, idx, src, axis=0):
    return tgt.at[idx].add(src)
def _segment_sum(src, seg, n):
    return jax.ops.segment_sum(src, seg, n)

kernel_name = 'mk_metaformer_d1_conv_nhwc128_115a66'

def setup_inputs(seed: int = 0):
    np.random.seed(seed)
    _w = jnp.asarray
    def _rec_inputs():
        import jax
        import jax.numpy as jnp
        _gk = jax.random.key(seed)
        x = 7.22e-05 + 1 * jax.random.normal(jax.random.fold_in(_gk, 1), (1, 256, 256, 128), jnp.float32)
        return x
    x = _rec_inputs()
    def _L0_conv_setup():
        import jax, jax.numpy as jnp
        import numpy as np
        D = 128
        C = 64
        H = 4
        L = 256
        N = 1
        EPS = 1e-05

        def _layernorm(x, gamma, beta):
            mu = jnp.mean(x, axis=-1, keepdims=True)
            var = jnp.mean(jnp.square(x - mu), axis=-1, keepdims=True)
            return (x - mu) * jax.lax.rsqrt(var + EPS) * gamma + beta
        key = jax.random.key(seed)
        ks = jax.random.split(key, 10)
        pair_rep = jax.random.normal(ks[0], (N, L, L, D), dtype=jnp.float32)
        mask = (jax.random.uniform(ks[1], (N, L, L)) < 0.9).astype(jnp.float32)
        s = 1.0 / np.sqrt(D)
        Wq = jax.random.normal(ks[2], (D, H * C), dtype=jnp.float32) * s
        Wk = jax.random.normal(ks[3], (D, H * C), dtype=jnp.float32) * s
        Wv = jax.random.normal(ks[4], (D, H * C), dtype=jnp.float32) * s
        Wb = jax.random.normal(ks[5], (D, H), dtype=jnp.float32) * s
        Wu = jax.random.normal(ks[6], (D, H * C), dtype=jnp.float32) * s
        bu = jnp.zeros((H * C,), dtype=jnp.float32)
        Wo = jax.random.normal(ks[7], (H * C, D), dtype=jnp.float32) / np.sqrt(H * C)
        bo = jnp.zeros((D,), dtype=jnp.float32)
        gamma = jnp.ones((D,), dtype=jnp.float32)
        beta = jnp.zeros((D,), dtype=jnp.float32)
        return dict(pair_rep=pair_rep, mask=mask, gamma=gamma, beta=beta, Wq=Wq, Wk=Wk, Wv=Wv, Wb=Wb, Wu=Wu, bu=bu, Wo=Wo, bo=bo)
    _L0_conv_all = _L0_conv_setup()
    _L0_conv_in = {k: v for k, v in _L0_conv_all.items() if k in ('mask', 'gamma', 'beta', 'Wq', 'Wk', 'Wv', 'Wb', 'Wu', 'bu', 'Wo', 'bo', )}
    del _L0_conv_all

    def _L0_ffn_setup():
        import jax, jax.numpy as jnp
        import numpy as np
        B, N, D, C, E, K = (8, 8192, 128, 128, 8, 2)
        key = jax.random.key(seed)
        k0, k1, k2 = jax.random.split(key, 3)
        x = jax.random.normal(k0, (B, N, D), dtype=jnp.float32)
        router_w = jax.random.normal(k1, (D, E), dtype=jnp.float32) * 0.05
        router_b = jnp.zeros((E,), dtype=jnp.float32)
        expert_w = jax.random.normal(k2, (E, D, C), dtype=jnp.float32) * (1.0 / np.sqrt(D))
        expert_b = jnp.zeros((E, C), dtype=jnp.float32)
        return {'x': x, 'router_w': router_w, 'router_b': router_b, 'expert_w': expert_w, 'expert_b': expert_b}
    _L0_ffn_all = _L0_ffn_setup()
    _L0_ffn_in = {k: v for k, v in _L0_ffn_all.items() if k in ('router_w', 'router_b', 'expert_w', 'expert_b', )}
    del _L0_ffn_all

    return {
        "x": x,
        "L0_conv_mask": _L0_conv_in["mask"],
        "L0_conv_gamma": _L0_conv_in["gamma"],
        "L0_conv_beta": _L0_conv_in["beta"],
        "L0_conv_Wq": _L0_conv_in["Wq"],
        "L0_conv_Wk": _L0_conv_in["Wk"],
        "L0_conv_Wv": _L0_conv_in["Wv"],
        "L0_conv_Wb": _L0_conv_in["Wb"],
        "L0_conv_Wu": _L0_conv_in["Wu"],
        "L0_conv_bu": _L0_conv_in["bu"],
        "L0_conv_Wo": _L0_conv_in["Wo"],
        "L0_conv_bo": _L0_conv_in["bo"],
        "L0_ffn_router_w": _L0_ffn_in["router_w"],
        "L0_ffn_router_b": _L0_ffn_in["router_b"],
        "L0_ffn_expert_w": _L0_ffn_in["expert_w"],
        "L0_ffn_expert_b": _L0_ffn_in["expert_b"],
    }

def reference(x, L0_conv_mask, L0_conv_gamma, L0_conv_beta, L0_conv_Wq, L0_conv_Wk, L0_conv_Wv, L0_conv_Wb, L0_conv_Wu, L0_conv_bu, L0_conv_Wo, L0_conv_bo, L0_ffn_router_w, L0_ffn_router_b, L0_ffn_expert_w, L0_ffn_expert_b):
    import jax
    import jax.numpy as jnp
    def _L0_conv_ref(pair_rep, mask, gamma, beta, Wq, Wk, Wv, Wb, Wu, bu, Wo, bo):
        import jax, jax.numpy as jnp
        import numpy as np
        D = 128
        C = 64
        H = 4
        L = 256
        N = 1
        EPS = 1e-05

        def _layernorm(x, gamma, beta):
            mu = jnp.mean(x, axis=-1, keepdims=True)
            var = jnp.mean(jnp.square(x - mu), axis=-1, keepdims=True)
            return (x - mu) * jax.lax.rsqrt(var + EPS) * gamma + beta
        x = _layernorm(pair_rep, gamma, beta)
        n, s, _, _ = x.shape
        q = x @ Wq * C ** (-0.5)
        q = q.reshape(n, s, s, H, C)
        k = (x @ Wk).reshape(n, s, s, H, C)
        v = (x @ Wv).reshape(n, s, s, H, C)
        dpa = jnp.einsum('nsqhc,nsvhc->nsqvh', k, q)
        pair_bias = x @ Wb
        bias = 1000000000.0 * (mask - 1.0)
        dpa = dpa + bias[:, None, :, :, None]
        attention = jax.nn.softmax(dpa + pair_bias[:, None], axis=3)
        out = jnp.einsum('nsqvh,nsvhc->nsqhc', attention, v)
        fu = jax.nn.sigmoid(x @ Wu + bu).reshape(n, s, s, H, C)
        out = out * fu
        out = out.reshape(n, s, s, H * C) @ Wo + bo
        out = out * mask[..., None]
        return out

    def _L0_ffn_ref(x, router_w, router_b, expert_w, expert_b):
        import jax, jax.numpy as jnp
        import numpy as np
        B, N, D, C, E, K = (8, 8192, 128, 128, 8, 2)
        router_probs = jax.nn.softmax(x @ router_w + router_b, axis=-1)
        top_p, top_i = jax.lax.top_k(router_probs, K)
        top_p = top_p / jnp.sum(top_p, axis=-1, keepdims=True)
        expert_out = jnp.einsum('bnd,edc->bnec', x, expert_w) + expert_b
        gathered = jnp.take_along_axis(expert_out, top_i[..., None], axis=2)
        return jnp.einsum('bnk,bnkc->bnc', top_p, gathered)

    def _gn(v, G=32, eps=1e-5):
        B_, H_, W_, C_ = v.shape
        g = v.reshape(B_, H_, W_, G, C_ // G)
        m = jnp.mean(g, axis=(1, 2, 4), keepdims=True)
        s = jnp.var(g, axis=(1, 2, 4), keepdims=True)
        return ((g - m) / jnp.sqrt(s + eps)).reshape(v.shape)

    def _ln_c(v, eps=1e-6):
        m = jnp.mean(v, axis=-1, keepdims=True)
        s = jnp.var(v, axis=-1, keepdims=True)
        return (v - m) / jnp.sqrt(s + eps)

    def _ln_t(v, eps=1e-5):
        m = jnp.mean(v, axis=-1, keepdims=True)
        s = jnp.var(v, axis=-1, keepdims=True)
        return (v - m) / jnp.sqrt(s + eps)

    def _to_tokens(v):
        B_, H_, W_, C_ = v.shape
        return v.reshape(B_, H_ * W_, C_)
    def _from_tokens(t, like):
        return t.reshape(like.shape)

    x = x + _L0_conv_ref(_ln_c(x), L0_conv_mask, L0_conv_gamma, L0_conv_beta, L0_conv_Wq, L0_conv_Wk, L0_conv_Wv, L0_conv_Wb, L0_conv_Wu, L0_conv_bu, L0_conv_Wo, L0_conv_bo)
    t = _to_tokens(x)
    t = t + _L0_ffn_ref(_ln_t(t), L0_ffn_router_w, L0_ffn_router_b, L0_ffn_expert_w, L0_ffn_expert_b)
    x = _from_tokens(t, x)
    return x


_drawn_inputs = setup_inputs


def setup_inputs(seed=0):
    import zlib

    import numpy as np

    out = dict(_drawn_inputs(seed))
    spreads = {'L0_conv_gamma': (1.0, 0.2),
     'L0_conv_beta': (0.0, 0.1),
     'L0_conv_bu': (0.0, 0.1),
     'L0_conv_bo': (0.0, 0.1),
     'L0_ffn_router_b': (0.0, 0.1),
     'L0_ffn_expert_b': (0.0, 0.1)}
    factors = {}
    for name, (base, spread) in spreads.items():
        noise = np.random.default_rng([zlib.crc32(name.encode()), seed]).standard_normal(out[name].shape)
        drawn = base * np.exp(spread * noise) if base else spread * noise
        out[name] = jnp.asarray(drawn.astype(out[name].dtype))
    for name, factor in factors.items():
        out[name] = (out[name] * factor).astype(out[name].dtype)
    return out
```

```python
from contextlib import ExitStack

import concourse.bass as bass
from concourse import mybir

ALU = mybir.AluOpType
ACT = mybir.ActivationFunctionType
F32 = mybir.dt.float32
F32R = mybir.dt.float32r
U32 = mybir.dt.uint32


def metaformer_kernel(nc, x, mask, gamma, beta, Wq, Wk, Wv, Wb, Wu, bu, Wo, bo,
                      router_w, router_b, expert_w, expert_b, eye, iota8, out):
    _, ROWS, L, D = x.shape
    HC = Wq.shape[1]
    H = Wb.shape[1]
    C = HC // H
    E = router_w.shape[1]
    P = 128
    T = L // P
    BLK = HC // P
    PAIRS = ROWS // 2
    SCALE = float(C) ** -0.5
    EPS_X, EPS_LN, EPS_T = 1e-6, 1e-5, 1e-5
    EXC = 3
    assert (D, T, BLK, H, C, E) == (128, 2, 2, 4, 64, 8)

    x_pair = x.rearrange("a (m r) (p t) c -> (a m) p r t c", r=2, t=T)
    x_row = x.rearrange("a r (p t) c -> (a r) p t c", t=T)
    out_row = out.rearrange("a r (p t) c -> (a r) p t c", t=T)

    with ExitStack() as ctx:
        def sb(name, shape, dt=F32):
            return ctx.enter_context(nc.sbuf_tensor(name, shape, dt))

        def sem(name):
            return ctx.enter_context(nc.semaphore(name))

        def sems(name, n):
            return [sem(f"{name}{k}") for k in range(n)]

        S = [ctx.enter_context(nc.psum_tensor(f"scores{h}", [P, 512], F32)) for h in range(H)]
        G = [ctx.enter_context(nc.psum_tensor(f"general{k}", [P, 512], F32)) for k in range(3)]
        O = ctx.enter_context(nc.psum_tensor("attended", [P, 512], F32))

        ident = sb("ident", [P, P])
        iota = sb("iota", [P, E])
        gam = sb("gam", [P, 1])
        bet = sb("bet", [P, 1])
        bu_half = sb("bu_half", [P, BLK])
        bo_rows = sb("bo_rows", [P, D])
        rb_rows = sb("rb_rows", [P, E])
        eb = sb("eb", [E, D])
        neg_half = sb("neg_half", [P, 4])
        stage_w = sb("stage_w", [P, 2, E * D])
        wb = sb("wb", [P, H])
        wo = sb("wo", [P, BLK, D])
        wq = [sb("wq_hi", [P, HC], F32R), sb("wq_lo", [P, HC], F32R)]
        wk = [sb("wk_hi", [P, HC], F32R), sb("wk_lo", [P, HC], F32R)]
        wv = [sb("wv_hi", [P, HC], F32R), sb("wv_lo", [P, HC], F32R)]
        wu = [sb("wu_hi", [P, HC], F32R), sb("wu_lo", [P, HC], F32R)]
        EW = E * D + E
        we = [sb("we_hi", [P, EW], F32R), sb("we_lo", [P, EW], F32R)]

        ln_table = sb("ln_table", [P, ROWS, 2 * T])
        biasT = sb("biasT", [P, T, H, ROWS])
        mask_q = sb("mask_q", [P, T, L])
        mask_neg = sb("mask_neg", [P, T, L])
        maskT = sb("maskT", [P, ROWS // 2, 2, T])
        neg_bias = sb("neg_bias", [P, H, T, L])

        x1p = sb("x1p", [P, 2, 2, T, D])
        bn1 = sb("bn1", [P, 2, 4, 6])
        mv1 = sb("mv1", [P, 2, 4, 2])
        ve1 = sb("ve1", [P, 2, 4])
        ln1 = sb("ln1", [P, 2, 2, 2, T])
        xn1 = sb("xn1", [P, 2, 2, T, D])
        xt1 = sb("xt1", [P, 2, 2 * L])

        xin = sb("xin", [P, 2, T, D])
        ln_row = sb("ln_row", [P, 2 * T])
        m_row = sb("m_row", [P, T])
        bom = sb("bom", [P, T, D])
        xb = sb("xb", [P, 2, T, D])
        xn = sb("xn", [P, 2, T, D])
        xt_f = sb("xt_f", [P, L])
        xt = [sb("xt_hi", [P, L], F32R), sb("xt_lo", [P, L], F32R)]
        q2 = [sb("q_hi", [P, BLK * L], F32R), sb("q_lo", [P, BLK * L], F32R)]
        k2 = [sb("k_hi", [P, BLK * L], F32R), sb("k_lo", [P, BLK * L], F32R)]
        v_s = sb("v_s", [P, T, HC])
        th_u = sb("th_u", [P, 2, BLK * L])
        prob = sb("prob", [P, H, T, L])
        neg_max = sb("neg_max", [P, H, T])
        sums = sb("sums", [P, H, T])
        rsum = sb("rsum", [P, H, T])
        pT = sb("pT", [P, H, T * L])
        on = sb("on", [P, T, HC])
        gated = sb("gated", [P, BLK * L])
        x1 = sb("x1", [P, T, D])
        bn2 = sb("bn2", [P, T, 6])
        mv2 = sb("mv2", [P, T, 2])
        ve2 = sb("ve2", [P, T])
        rstd2 = sb("rstd2", [P, T])
        tn = sb("tn", [P, T, D])
        tt = [sb("tt_hi", [P, L], F32R), sb("tt_lo", [P, L], F32R)]
        lg = sb("lg", [P, T, E])
        top = sb("top", [P, T, 8])
        topi = sb("topi", [P, T, 8], U32)
        topf = sb("topf", [P, T, 2])
        gap = sb("gap", [P, T])
        th_g = sb("th_g", [P, T])
        w1 = sb("w1", [P, T])
        w2 = sb("w2", [P, T])
        oh = sb("oh", [P, T, 2, E])
        wt = sb("wt", [P, T, E])
        wT = sb("wT", [E, L])
        Y = sb("Y", [P, T, E * D])
        x1w = sb("x1w", [P, T, D])
        outb = sb("outb", [P, 2, T, D])

        w_in = sem("w_in")
        small_in = sem("small_in")
        mask_in = sem("mask_in")
        consts = sem("consts")
        scaled = sem("scaled")
        hi_made = sem("hi_made")
        staged = sem("staged")
        pair_in = sems("pair_in", 2)
        bn1_s = sem("bn1_s")
        mv1_s = sem("mv1_s")
        ve1_s = sem("ve1_s")
        rs1_s = sem("rs1_s")
        nb1_s = sem("nb1_s")
        tab_s = sem("tab_s")
        xn1_dve = sem("xn1_dve")
        xn1_act = sem("xn1_act")
        xt1_ready = sem("xt1_ready")
        xt1_s = sem("xt1_s")
        pb_ready = sem("pb_ready")
        bt_s = sem("bt_s")
        bt_ready = sem("bt_ready")
        mt_ready = sem("mt_ready")
        mneg_s = sem("mneg_s")
        mt_s = sem("mt_s")
        tables = sem("tables")
        x_in = sems("x_in", 2)
        stored = sems("stored", 2)
        sc_ready = sems("sc_ready", 2)
        wo_ready = sem("wo_ready")
        xt_ready = sem("xt_ready")
        pt_ready = sems("pt_ready", H)
        q_ready = sem("q_ready")
        k_ready = sem("k_ready")
        u_ready = sem("u_ready")
        v_ready = sem("v_ready")
        tt_ready = sem("tt_ready")
        pv_ready = sem("pv_ready")
        ec_ready = sems("ec_ready", T)
        ea_ready = sems("ea_ready", T)
        eb_ready = sems("eb_ready", T)
        wT_ready = sem("wT_ready")
        wb_ready = sem("wb_ready")
        ot_ready = sem("ot_ready")
        exp_s = sems("exp_s", H)
        xtf_s = sem("xtf_s")
        pT_s = sems("pT_s", H)
        qhi_s = sem("qhi_s")
        khi_s = sem("khi_s")
        tthi_s = sem("tthi_s")
        thg_s = sem("thg_s")
        wT_s = sem("wT_s")
        thu_s = sem("thu_s")
        v_s_s = sem("v_s_s")
        lgt_s = sems("lgt_s", 2 * H)
        x1_s = sem("x1_s")
        bn2_s = sem("bn2_s")
        mv2_s = sem("mv2_s")
        ve2_s = sem("ve2_s")
        xthi_s = sem("xthi_s")
        tn_s = sem("tn_s")
        qlo_s = sem("qlo_s")
        klo_s = sem("klo_s")
        ttlo_s = sem("ttlo_s")
        rsum_s = sem("rsum_s")
        lg_s = sem("lg_s")
        top_s = sem("top_s")
        topi_s = sem("topi_s")
        on_s = sem("on_s")
        yc_s = sems("yc_s", T)
        ya_s = sems("ya_s", T)
        yb_s = sems("yb_s", T)
        x1w_s = sem("x1w_s")
        gated_s = sem("gated_s")
        mrow_s = sem("mrow_s")
        bom_s = sem("bom_s")
        xb_s = sem("xb_s")
        lnrow_s = sem("lnrow_s")
        xn_s = sem("xn_s")
        rstd2_s = sem("rstd2_s")
        xtlo_s = sem("xtlo_s")
        gap_s = sem("gap_s")
        w12_s = sem("w12_s")
        oh_s = sem("oh_s")
        wt_s = sem("wt_s")
        half_s = sem("half_s")
        quarter_s = sem("quarter_s")
        ysum_s = sem("ysum_s")
        out_s = sem("out_s")

        def at(j, off):
            return 2 * j + off

        def till(eng, s, n):
            if isinstance(n, int) and n <= 0:
                return
            eng.wait_ge(s, n)

        def till_alone(eng, s, n):
            till(eng, s, n)
            eng.nop(nofuse=True)

        def one(ap, r):
            return ap[r] if isinstance(r, int) else ap[bass.ds(r, 1)].squeeze(0)

        def drive1(eng, step):
            for m in range(4):
                step(m // 2, m % 2, m)
            with eng.Fori(2, PAIRS // 2) as j:
                step(j, 0, None)
                step(j, 1, None)
            for m in range(PAIRS, PAIRS + 3):
                step(m // 2, m % 2, m)

        def stages1(m):
            return [m is None or 0 <= m - k < PAIRS for k in range(4)]

        def drive2(eng, step):
            for i in range(-1, 2):
                step(i // 2, i % 2, i)
            with eng.Fori(1, ROWS // 2 - 1) as j:
                step(j, 0, None)
                step(j, 1, None)
            for i in range(ROWS - 2, ROWS + 1):
                step(i // 2, i % 2, i)

        def stages2(i):
            return [i is None or 0 <= i + 1 - k < ROWS for k in range(3)]

        block = ctx.enter_context(nc.Block())

        @block.sync
        def _(sp):
            for k, w in enumerate((Wq, Wk, Wv, Wu)):
                sp.dma_start(stage_w[:, 0, k * HC:(k + 1) * HC], w).then_inc(w_in, 16)
            sp.dma_start(stage_w[:, 1, :].rearrange("p (e c) -> p e c", e=E),
                         expert_w.rearrange("e d c -> d e c")).then_inc(w_in, 16)
            for dst, src in ((ident[:], eye), (iota[:], iota8),
                             (gam[:], gamma.rearrange("(d a) -> d a", a=1)),
                             (bet[:], beta.rearrange("(d a) -> d a", a=1)),
                             (bo_rows[:], bo.partition_broadcast(P)),
                             (rb_rows[:], router_b.partition_broadcast(P)),
                             (eb[:], expert_b), (wb[:], Wb),
                             (wo[:], Wo.rearrange("(b p) d -> p b d", p=P))):
                sp.dma_start(dst, src).then_inc(small_in, 16)
            with nc.allow_non_contiguous_dma(reason="256 biases"):
                sp.dma_start(bu_half[:], bu.rearrange("(b p) -> p b", p=P)).then_inc(small_in, 16)
            sp.dma_start(mask_q[:], mask.rearrange("a (p t) v -> p (a t) v", t=T)).then_inc(mask_in, 16)

            def step1(j, off, m):
                if not stages1(m)[0]:
                    return
                till(sp, xn1_dve, at(j, off) - 1)
                till(sp, xn1_act, at(j, off) - 1)
                sp.dma_start(x1p[:, off], one(x_pair, at(j, off))).then_inc(pair_in[off], 16)
                if m == 3:
                    sp.wait_ge(staged, 1)
                    sp.dma_start(stage_w[:, 0, 0:E], router_w).then_inc(w_in, 16)
            drive1(sp, step1)

            for r in range(2):
                sp.dma_start(xin[:, r], x_row[r]).then_inc(x_in[r], 16)

            def step2(j, off, i):
                a, b, c = stages2(i)
                if b and (i is None or i + 2 < ROWS):
                    till(sp, xb_s, at(j, off) + 1)
                    sp.dma_start(xin[:, off], one(x_row, at(j, off) + 2)).then_inc(x_in[off], 16)
                if c:
                    till(sp, out_s, at(j, off))
                    sp.dma_start(one(out_row, at(j, off) - 1), outb[:, 1 - off]).then_inc(stored[1 - off], 16)
            drive2(sp, step2)
            for k in range(2):
                sp.wait_ge(stored[k], 16 * ROWS // 2)

        @block.tensor
        def _(pe):
            def transpose(dst, src):
                return nc.tensor.transpose(dst, src, ident[:])

            pe.wait_ge(small_in, 16 * 10)

            def step1(j, off, m):
                _, _, s2, s3 = stages1(m)
                if s2:
                    n = at(j, off) - 1
                    till(pe, xn1_dve, n)
                    till(pe, xn1_act, n)
                    till(pe, xt1_s, n - 2)
                    for r in range(2):
                        for t in range(T):
                            mm = transpose(G[off][:, (r * T + t) * P:(r * T + t + 1) * P], xn1[:, off, r, t])
                    mm.then_inc(xt1_ready, 1)
                if s3:
                    n = at(j, off) - 2
                    till(pe, xt1_s, n)
                    till(pe, bt_s, n - 2)
                    for k in range(2 * T):
                        mm = nc.tensor.matmul(S[1 - off][:, k * H:(k + 1) * H], xt1[:, 1 - off, k * P:(k + 1) * P],
                                              wb[:], start=True, stop=True)
                    mm.then_inc(pb_ready, 1)
            drive1(pe, step1)

            pe.wait_ge(bt_s, PAIRS)
            for h in range(H):
                for a in range(T):
                    for t in range(T):
                        mm = transpose(S[h][:, (a * T + t) * P:(a * T + t + 1) * P], biasT[:, t, h, a::T])
                mm.then_inc(bt_ready, 1)
            pe.wait_ge(mask_in, 16)
            for a in range(2):
                for b in range(T):
                    mm = transpose(O[:, (a * T + b) * P:(a * T + b + 1) * P], mask_q[:, a, b::T])
            mm.then_inc(mt_ready, 1)
            pe.wait_ge(tables, 1)

            def split_product(dst, left, right, lo_left=None, lo_right=None):
                nc.tensor.matmul(dst, left[0], right[0], start=True, stop=False)
                if lo_left:
                    pe.wait_ge(*lo_left)
                nc.tensor.matmul(dst, left[1], right[0], start=False, stop=False)
                if lo_right:
                    pe.wait_ge(*lo_right)
                return nc.tensor.matmul(dst, left[0], right[1], start=False, stop=True)

            def step2(j, off, i):
                A, B, Cc = stages2(i)
                row = at(j, off)
                na, nb, nc_ = row + 2, row + 1, row

                def scores(pair):
                    if pair == 0:
                        till(pe, qhi_s, nb)
                        till(pe, khi_s, nb)
                        till(pe, qlo_s, nb)
                        till(pe, klo_s, nb)
                    till(pe, ya_s[pair], nb - 2)
                    till(pe, yb_s[pair], nb - 2)
                    if pair == 0:
                        till(pe, pT_s[H - 1], nb - 1)
                    for a in range(T):
                        for kp, qp in ((0, 0), (1, 0), (0, 1)):
                            for e in range(2):
                                rows = slice(e * C, (e + 1) * C)
                                mm = nc.tensor.matmul(
                                    S[2 * pair + e][:, a * L:(a + 1) * L],
                                    k2[kp][rows, pair * L + a * P:pair * L + (a + 1) * P],
                                    q2[qp][rows, pair * L:(pair + 1) * L],
                                    start=(kp, qp) == (0, 0), stop=(kp, qp) == (0, 1))
                    mm.then_inc(sc_ready[pair], 1)

                def probs_transposed(h):
                    till(pe, exp_s[h], nb)
                    for a in range(T):
                        for t in range(T):
                            mm = transpose(S[h][:, t * L + a * P:t * L + (a + 1) * P],
                                           prob[:, h, a, t * P:(t + 1) * P])
                    mm.then_inc(pt_ready[h], 1)

                def attend(h):
                    till(pe, pT_s[h], nb)
                    for a in range(T):
                        for t in range(T):
                            mm = nc.tensor.matmul(O[:, a * HC + h * C:a * HC + (h + 1) * C],
                                                  pT[:, h, t * L + a * P:t * L + (a + 1) * P],
                                                  v_s[:, t, h * C:(h + 1) * C], start=t == 0, stop=t == T - 1)
                    if h == H - 1:
                        mm.then_inc(pv_ready, 1)

                def project_rows(bank, w, ready, lo=None):
                    for b in range(BLK):
                        cols = slice(b * P, (b + 1) * P)
                        mm = split_product(bank[:, b * L:(b + 1) * L], [w[0][:, cols], w[1][:, cols]],
                                           [xt[0][:], xt[1][:]], lo_right=lo if b == 0 else None)
                    mm.then_inc(ready, 1)

                def experts(bank, t, first, width, ready):
                    cols = slice(first * D, first * D + width)
                    toks = slice(t * P, (t + 1) * P)
                    split_product(bank[:, 0:width], [tt[0][:, toks], tt[1][:, toks]],
                                  [we[0][:, cols], we[1][:, cols]]).then_inc(ready, 1)

                if B:
                    scores(0)
                if Cc:
                    till(pe, gated_s, nc_)
                    if B:
                        till(pe, v_s_s, nb)
                    for a in range(T):
                        for b in range(BLK):
                            mm = nc.tensor.matmul(G[0][:, a * D:(a + 1) * D],
                                                  gated[:, b * L + a * P:b * L + (a + 1) * P], wo[:, b, :],
                                                  start=b == 0, stop=b == BLK - 1)
                    mm.then_inc(wo_ready, 1)
                if B:
                    scores(1)
                if A:
                    till(pe, xn_s, na)
                    till(pe, gated_s, nc_)
                    for t in range(T):
                        mm = transpose(G[1][:, t * P:(t + 1) * P], xn[:, 1 - off, t])
                    mm.then_inc(xt_ready, 1)
                if B:
                    probs_transposed(0)
                    probs_transposed(1)
                if A:
                    till(pe, thu_s, nb)
                    till(pe, xthi_s, na)
                    project_rows(G[2], wq, q_ready, lo=(xtlo_s, na))
                    if Cc:
                        till(pe, x1_s, nc_)
                    elif B:
                        till(pe, v_s_s, nb)
                    project_rows(G[0], wk, k_ready)
                if Cc:
                    till(pe, tn_s, nc_)
                    if A:
                        till(pe, xtf_s, na)
                    for t in range(T):
                        mm = transpose(G[1][:, t * P:(t + 1) * P], tn[:, t])
                    mm.then_inc(tt_ready, 1)
                if B:
                    probs_transposed(2)
                    probs_transposed(3)
                    till(pe, on_s, nb - 1)
                    attend(0)
                    attend(1)
                if Cc:
                    till(pe, tthi_s, nc_)
                    till(pe, ttlo_s, nc_)
                    experts(G[1], 0, 2 * EXC, 2 * D + E, ec_ready[0])
                    if A:
                        till(pe, qlo_s, na)
                    experts(G[2], 1, 2 * EXC, 2 * D + E, ec_ready[1])
                if B:
                    attend(2)
                    attend(3)
                if Cc:
                    for t in range(T):
                        for s in range(2):
                            if B:
                                till(pe, pT_s[2 * t + s], nb)
                            experts(S[2 * t + s], t, EXC * s, EXC * D, (ea_ready, eb_ready)[s][t])
                    till(pe, wt_s, nc_)
                    if A:
                        till(pe, klo_s, na)
                    for t in range(T):
                        mm = transpose(G[0][0:E, t * P:(t + 1) * P], wt[:, t])
                    mm.then_inc(wT_ready, 1)
                    till(pe, wT_s, nc_)
                    for t in range(T):
                        mm = nc.tensor.matmul(G[0][:, t * D:(t + 1) * D], wT[:, t * P:(t + 1) * P], eb[:],
                                              start=True, stop=True)
                    mm.then_inc(wb_ready, 1)
                if A:
                    if Cc:
                        till(pe, yc_s[1], nc_)
                    else:
                        till(pe, qlo_s, na)
                    project_rows(G[2], wu, u_ready)
                    if Cc:
                        till(pe, x1w_s, nc_)
                    else:
                        till(pe, klo_s, na)
                    for t in range(T):
                        toks = slice(t * P, (t + 1) * P)
                        mm = split_product(G[0][:, t * HC:(t + 1) * HC], [xt[0][:, toks], xt[1][:, toks]],
                                           [wv[0][:], wv[1][:]])
                    mm.then_inc(v_ready, 1)
                if B:
                    till(pe, on_s, nb)
                    if Cc:
                        till(pe, yc_s[0], nc_)
                    elif A:
                        till(pe, xtf_s, na)
                    for b in range(BLK):
                        for a in range(T):
                            mm = transpose(G[1][:, b * L + a * P:b * L + (a + 1) * P], on[:, a, b * P:(b + 1) * P])
                    mm.then_inc(ot_ready, 1)
            drive2(pe, step2)

        @block.scalar
        def _(act):
            def step1(j, off, m):
                _, s1, s2, _ = stages1(m)
                if s1:
                    n = at(j, off)
                    par = 1 - off
                    till(act, nb1_s, n)
                    till(act, xt1_ready, n - 2)
                    for t in range(T):
                        last = nc.scalar.activation(xn1[:, par, 1, t], x1p[:, par, 1, t], ACT.Identity,
                                                    bias=ln1[:, par, 1, 1, t:t + 1], scale=ln1[:, par, 1, 0, t:t + 1])
                    last.then_inc(xn1_act, 1)
                if s2:
                    n = at(j, off) - 1
                    till(act, xt1_ready, n)
                    till(act, pb_ready, n - 2)
                    nc.scalar.activation(xt1[:, off], G[off][:], ACT.Identity, bias=bet[:], scale=gam[:])\
                        .then_inc(xt1_s, 1)
            act.wait_ge(small_in, 16 * 10)
            drive1(act, step1)
            act.wait_ge(tables, 1)

            def step2(j, off, i):
                A, B, Cc = stages2(i)
                row = at(j, off)
                na, nb, nc_ = row + 2, row + 1, row

                def exps(pair):
                    for a in range(T):
                        for h in (2 * pair, 2 * pair + 1):
                            till(act, lgt_s[2 * h + a], nb)
                            if pair == 0 and a == 0 and h == 0:
                                till(act, rsum_s, nb - 1)
                            ex = nc.scalar.activation(prob[:, h, a], prob[:, h, a], ACT.Exp, scale=-1.0,
                                                      bias=neg_max[:, h, a:a + 1], accum_out=sums[:, h, a:a + 1])
                            if a == T - 1:
                                ex.then_inc(exp_s[h], 1)

                def probs_out(h):
                    till(act, pt_ready[h], nb)
                    till(act, pv_ready, nb - 1)
                    nc.scalar.copy(pT[:, h], S[h][:]).then_inc(pT_s[h], 1)

                if B:
                    exps(0)
                if A:
                    till(act, xt_ready, na)
                    till(act, xtlo_s, na - 1)
                    nc.scalar.activation(xt_f[:], G[1][:, 0:L], ACT.Identity, bias=bet[:], scale=gam[:])\
                        .then_inc(xtf_s, 1)
                if B:
                    exps(1)
                    probs_out(0)
                    probs_out(1)
                if A:
                    till(act, q_ready, na)
                    till(act, sc_ready[1], nb)
                    nc.scalar.copy(q2[0][:], G[2][:]).then_inc(qhi_s, 1)
                    till(act, k_ready, na)
                    nc.scalar.copy(k2[0][:], G[0][:]).then_inc(khi_s, 1)
                if Cc:
                    till(act, tt_ready, nc_)
                    till(act, eb_ready[1], nc_ - 1)
                    nc.scalar.copy(tt[0][:], G[1][:, 0:L]).then_inc(tthi_s, 1)
                if B:
                    probs_out(2)
                    probs_out(3)
                if Cc:
                    till(act, gap_s, nc_)
                    nc.scalar.activation(th_g[:], gap[:], ACT.Tanh, scale=0.5).then_inc(thg_s, 1)
                    till(act, wT_ready, nc_)
                    till(act, wb_ready, nc_ - 1)
                    nc.scalar.copy(wT[:], G[0][0:E, 0:L]).then_inc(wT_s, 1)
                if A:
                    till(act, u_ready, na)
                    till(act, gated_s, nc_)
                    for b in range(BLK):
                        last = nc.scalar.activation(th_u[:, 1 - off, b * L:(b + 1) * L], G[2][:, b * L:(b + 1) * L],
                                                    ACT.Tanh, bias=bu_half[:, b:b + 1], scale=0.5)
                    last.then_inc(thu_s, 1)
                    till(act, v_ready, na)
                    till(act, pv_ready, nb)
                    nc.scalar.copy(v_s[:].rearrange("p t c -> p (t c)"), G[0][:]).then_inc(v_s_s, 1)
            drive2(act, step2)

        @block.vector
        def _(dve):
            V = nc.vector
            V.memset(neg_half[:], -0.5).then_inc(consts, 1)
            dve.wait_ge(small_in, 16 * 10)
            V.tensor_scalar(bu_half[:], bu_half[:], 0.5, None, ALU.mult).then_inc(scaled, 1)
            V.tensor_scalar(wo[:], wo[:], 0.5, None, ALU.mult).then_inc(scaled, 1)
            dve.wait_ge(w_in, 16 * 5)
            V.tensor_scalar(stage_w[:, 0, 0:HC], stage_w[:, 0, 0:HC], -SCALE, None, ALU.mult).then_inc(scaled, 1)
            dve.wait_ge(scaled, 3)
            for k, w in enumerate((wq, wk, wv, wu)):
                V.tensor_copy(w[0][:], stage_w[:, 0, k * HC:(k + 1) * HC]).then_inc(hi_made, 1)
            V.tensor_copy(we[0][:, 0:E * D], stage_w[:, 1, :]).then_inc(hi_made, 1)
            dve.wait_ge(hi_made, 5)
            for k, w in enumerate((wq, wk, wv, wu)):
                lo = V.tensor_tensor(w[1][:], stage_w[:, 0, k * HC:(k + 1) * HC], w[0][:].bitcast(F32), ALU.subtract)
            lo.then_inc(staged, 1)
            V.tensor_tensor(we[1][:, 0:E * D], stage_w[:, 1, :], we[0][:, 0:E * D].bitcast(F32),
                            ALU.subtract).then_inc(staged, 1)

            def step1(j, off, m):
                s0, s1, _, s3 = stages1(m)
                if s0:
                    n = at(j, off) + 1
                    half = (j + 1) * 16
                    till(dve, pair_in[off], half)
                    for k in range(4):
                        last = V.bn_stats(bn1[:, off, k], x1p[:, off, k // 2, k % 2])
                    last.then_inc(bn1_s, 1)
                    till_alone(dve, bn1_s, n)
                    for k in range(4):
                        last = V.bn_aggr(mv1[:, off, k], bn1[:, off, k])
                    last.then_inc(mv1_s, 1)
                    dve.wait_ge(mv1_s, n)
                    V.tensor_scalar(ve1[:, off], mv1[:, off, :, 1], 1.0 + EPS_LN, EPS_X * EPS_LN,
                                    ALU.mult, ALU.add).then_inc(ve1_s, 1)
                if s1:
                    n = at(j, off)
                    par = 1 - off
                    till(dve, rs1_s, n)
                    V.scalar_tensor_tensor(ln1[:, par, :, 1, :], mv1[:, par, :, 0].rearrange("p (r t) -> p r t", r=2),
                                           -1.0, ln1[:, par, :, 0, :], ALU.mult, ALU.mult).then_inc(nb1_s, 1)
                    till(dve, nb1_s, n)
                    till(dve, xt1_ready, n - 2)
                    for t in range(T):
                        last = V.tensor_scalar(xn1[:, par, 0, t], x1p[:, par, 0, t], ln1[:, par, 0, 0, t:t + 1],
                                               ln1[:, par, 0, 1, t:t + 1], ALU.mult, ALU.add)
                    last.then_inc(xn1_dve, 1)
                    rows = slice(0, 0)
                    first = 2 * (n - 1)
                    dst = ln_table[:, bass.ds(first, 2), :]
                    V.tensor_copy(dst, ln1[:, par].rearrange("p r k t -> p r (k t)")).then_inc(tab_s, 1)
                if s3:
                    n = at(j, off) - 2
                    till(dve, pb_ready, n)
                    V.tensor_copy(biasT[:, :, :, bass.ds(2 * (n - 1), 2)],
                                  S[1 - off][:, 0:2 * T * H].rearrange("p (r t h) -> p t h r", r=2, t=T))\
                        .then_inc(bt_s, 1)
                if m == 3:
                    dve.wait_ge(w_in, 16 * 6)
                    V.tensor_copy(we[0][:, E * D:EW], stage_w[:, 0, 0:E]).then_inc(hi_made, 1)
                    dve.wait_ge(hi_made, 6)
                    V.tensor_tensor(we[1][:, E * D:EW], stage_w[:, 0, 0:E], we[0][:, E * D:EW].bitcast(F32),
                                    ALU.subtract).then_inc(staged, 1)
            drive1(dve, step1)

            dve.wait_ge(mask_in, 16)
            V.tensor_scalar(mask_neg[:].rearrange("p a (t v) -> p a t v", t=T),
                            mask_q[:].rearrange("p a (v t) -> p a t v", t=T),
                            -1.0, -1.0e9, ALU.add, ALU.mult).then_inc(mneg_s, 1)
            dve.wait_ge(mneg_s, 1)
            for h in range(H):
                dve.wait_ge(bt_ready, h + 1)
                V.tensor_tensor(neg_bias[:, h].rearrange("p a v -> p (a v)"),
                                mask_neg[:].rearrange("p a v -> p (a v)"), S[h][:], ALU.subtract)\
                    .then_inc(mt_s, 1)
            dve.wait_ge(mt_ready, 1)
            for b in range(T):
                V.tensor_copy(maskT[:, :, :, b],
                              O[:].rearrange("p (a b s) -> p b s a", a=2, b=T)[:, b]).then_inc(mt_s, 1)
            dve.wait_ge(mt_s, H + T)
            dve.wait_ge(staged, 3)
            dve.wait_ge(scaled, 3)
            V.memset(neg_half[:], -0.5).then_inc(tables, 1)

            def step2(j, off, i):
                A, B, Cc = stages2(i)
                row = at(j, off)
                na, nb, nc_ = row + 2, row + 1, row

                def logits(h, a):
                    till(dve, sc_ready[h // 2], nb)
                    till_alone(dve, pt_ready[h], nb - 1)
                    V.tensor_tensor_reduce(prob[:, h, a], S[h][:, a * L:(a + 1) * L], neg_bias[:, h, a], 1.0, 0.0,
                                           ALU.add, ALU.min, neg_max[:, h, a:a + 1]).then_inc(lgt_s[2 * h + a], 1)

                if B:
                    for a in range(T):
                        for h in (0, 1):
                            logits(h, a)
                if Cc:
                    till(dve, wo_ready, nc_)
                    till(dve, xb_s, nc_)
                    till(dve, x1w_s, nc_ - 1)
                    mrow = maskT[:].rearrange("p s a t -> p (s a) t")
                    for t in range(T):
                        last = V.scalar_tensor_tensor(x1[:, t], G[0][:, t * D:(t + 1) * D],
                                                      mrow[:, bass.ds(row - 1, 1), t], xb[:, 1 - off, t],
                                                      ALU.mult, ALU.add)
                    last.then_inc(x1_s, 1)
                    till(dve, x1_s, nc_)
                    for t in range(T):
                        last = V.bn_stats(bn2[:, t], x1[:, t])
                    last.then_inc(bn2_s, 1)
                if B:
                    logits(2, 0)
                if Cc:
                    till_alone(dve, bn2_s, nc_)
                    for t in range(T):
                        last = V.bn_aggr(mv2[:, t], bn2[:, t])
                    last.then_inc(mv2_s, 1)
                if B:
                    logits(3, 0)
                if Cc:
                    till(dve, mv2_s, nc_)
                    V.tensor_scalar(ve2[:], mv2[:, :, 1], EPS_T, None, ALU.add).then_inc(ve2_s, 1)
                if A:
                    till(dve, xtf_s, na)
                    till(dve, v_ready, na - 1)
                    V.tensor_copy(xt[0][:], xt_f[:]).then_inc(xthi_s, 1)
                if B:
                    logits(2, 1)
                    logits(3, 1)
                if Cc:
                    till(dve, rstd2_s, nc_)
                    till(dve, tt_ready, nc_ - 1)
                    for t in range(T):
                        last = V.tensor_scalar(tn[:, t], x1[:, t], mv2[:, t, 0:1], rstd2[:, t:t + 1],
                                               ALU.subtract, ALU.mult)
                    last.then_inc(tn_s, 1)
                if A:
                    till(dve, qhi_s, na)
                    V.tensor_tensor(q2[1][:], G[2][:], q2[0][:].bitcast(F32), ALU.subtract).then_inc(qlo_s, 1)
                    till(dve, khi_s, na)
                    V.tensor_tensor(k2[1][:], G[0][:], k2[0][:].bitcast(F32), ALU.subtract).then_inc(klo_s, 1)
                if Cc:
                    till(dve, tthi_s, nc_)
                    V.tensor_tensor(tt[1][:], G[1][:, 0:L], tt[0][:].bitcast(F32), ALU.subtract).then_inc(ttlo_s, 1)
                if B:
                    till(dve, exp_s[H - 1], nb)
                    till(dve, on_s, nb - 1)
                    V.reciprocal(rsum[:], sums[:]).then_inc(rsum_s, 1)
                if Cc:
                    for t in range(T):
                        till(dve, ec_ready[t], nc_)
                        last = V.tensor_tensor(lg[:, t], G[1 + t][:, 2 * D:2 * D + E], rb_rows[:], ALU.add)
                    last.then_inc(lg_s, 1)
                    till(dve, lg_s, nc_)
                    till_alone(dve, gap_s, nc_ - 1)
                    for t in range(T):
                        last = V.max(top[:, t], lg[:, t])
                    last.then_inc(top_s, 1)
                    till_alone(dve, top_s, nc_)
                    for t in range(T):
                        last = V.max_index(topi[:, t], top[:, t], lg[:, t])
                    last.then_inc(topi_s, 1)
                if B:
                    till(dve, pv_ready, nb)
                    till(dve, rsum_s, nb)
                    till(dve, ot_ready, nb - 1)
                    V.tensor_tensor(on[:].rearrange("p t (h c) -> p t h c", h=H),
                                    O[:].rearrange("p (t h c) -> p t h c", t=T, h=H),
                                    rsum[:].rearrange("p h t -> p t h").unsqueeze(3).to_broadcast([P, T, H, C]),
                                    ALU.mult).then_inc(on_s, 1)
                if Cc:
                    def weigh(bank, t, first, n, ready, done):
                        till(dve, ready, nc_)
                        V.tensor_tensor(Y[:, t, first * D:(first + n) * D].rearrange("p (e c) -> p e c", e=n),
                                        bank[:, 0:n * D].rearrange("p (e c) -> p e c", e=n),
                                        wt[:, t, first:first + n].unsqueeze(2).to_broadcast([P, n, D]),
                                        ALU.mult).then_inc(done, 1)
                    till(dve, wt_s, nc_)
                    till(dve, ysum_s, nc_ - 1)
                    for t in range(T):
                        weigh(G[1 + t], t, 2 * EXC, 2, ec_ready[t], yc_s[t])
                        weigh(S[2 * t], t, 0, EXC, ea_ready[t], ya_s[t])
                        weigh(S[2 * t + 1], t, EXC, EXC, eb_ready[t], yb_s[t])
                    till(dve, wb_ready, nc_)
                    till(dve, out_s, nc_ - 1)
                    V.tensor_tensor(x1w[:].rearrange("p t c -> p (t c)"), G[0][:, 0:T * D],
                                    x1[:].rearrange("p t c -> p (t c)"), ALU.add).then_inc(x1w_s, 1)
                if B:
                    till(dve, ot_ready, nb)
                    till(dve, thu_s, nb)
                    till(dve, wo_ready, nb - 1)
                    V.scalar_tensor_tensor(gated[:], th_u[:, off], 1.0, G[1][:], ALU.add, ALU.mult)\
                        .then_inc(gated_s, 1)
            drive2(dve, step2)

        @block.gpsimd
        def _(pool):
            Q = nc.gpsimd
            pool.wait_ge(consts, 1)

            def step1(j, off, m):
                if stages1(m)[0]:
                    n = at(j, off) + 1
                    till(pool, ve1_s, n)
                    till(pool, xn1_act, n - 2)
                    till(pool, xn1_dve, n - 2)
                    till(pool, tab_s, n - 2)
                    Q.tensor_tensor(ln1[:, off, :, 0, :], ve1[:, off].rearrange("p (r t) -> p r t", r=2),
                                    neg_half[:].rearrange("p (r t) -> p r t", r=2), ALU.pow).then_inc(rs1_s, 1)
            drive1(pool, step1)
            pool.wait_ge(tables, 1)
            pool.wait_ge(tab_s, PAIRS)

            def normalise(j, off, par, n):
                row = n - 1
                till(pool, x_in[par], 16 * (j + (off + 2) // 2) + 16)
                till_alone(pool, xn_s, n - 1)
                src = ln_table[:, row, :] if isinstance(row, int) else ln_table[:, bass.ds(row, 1), :].squeeze(1)
                Q.tensor_copy(ln_row[:], src).then_inc(lnrow_s, 1)
                till(pool, lnrow_s, n)
                till_alone(pool, xt_ready, n - 2)
                for t in range(T):
                    last = Q.tensor_scalar(xn[:, par, t], xin[:, par, t], ln_row[:, t:t + 1],
                                           ln_row[:, T + t:T + t + 1], ALU.mult, ALU.add)
                last.then_inc(xn_s, 1)

            def step2(j, off, i):
                A, B, Cc = stages2(i)
                row = at(j, off)
                na, nb, nc_ = row + 2, row + 1, row
                if i == -1:
                    normalise(-1, 0, 0, 1)
                if B:
                    till_alone(pool, bom_s, nb - 1)
                    mrow = maskT[:].rearrange("p s a t -> p (s a) t")
                    src = mrow[:, row, :] if isinstance(row, int) else mrow[:, bass.ds(row, 1), :].squeeze(1)
                    Q.tensor_copy(m_row[:], src).then_inc(mrow_s, 1)
                    till(pool, mrow_s, nb)
                    till_alone(pool, xb_s, nb - 1)
                    for t in range(T):
                        last = Q.tensor_scalar(bom[:, t], bo_rows[:], m_row[:, t:t + 1], 1.0, ALU.mult, ALU.mult)
                    last.then_inc(bom_s, 1)
                    till(pool, bom_s, nb)
                    till(pool, x1_s, nb - 2)
                    Q.tensor_tensor(xb[:, off], xin[:, off], bom[:], ALU.add).then_inc(xb_s, 1)
                if Cc:
                    till(pool, ve2_s, nc_)
                    till(pool, tn_s, nc_ - 1)
                    Q.tensor_tensor(rstd2[:], ve2[:], neg_half[:, 0:T], ALU.pow).then_inc(rstd2_s, 1)
                if A:
                    till(pool, xthi_s, na)
                    Q.tensor_tensor(xt[1][:], xt_f[:], xt[0][:].bitcast(F32), ALU.subtract).then_inc(xtlo_s, 1)
                if Cc:
                    till(pool, top_s, nc_)
                    till(pool, thg_s, nc_ - 1)
                    Q.tensor_tensor(gap[:], top[:, :, 0], top[:, :, 1], ALU.subtract).then_inc(gap_s, 1)
                    till(pool, topi_s, nc_)
                    till_alone(pool, oh_s, nc_ - 1)
                    Q.tensor_copy(topf[:], topi[:, :, 0:2])
                    till_alone(pool, thg_s, nc_)
                    Q.tensor_scalar(w1[:], th_g[:], 0.5, 0.5, ALU.mult, ALU.add)
                    Q.tensor_scalar(w2[:], th_g[:], -0.5, 0.5, ALU.mult, ALU.add).then_inc(w12_s, 1)
                    till(pool, w12_s, nc_)
                    till_alone(pool, wt_s, nc_ - 1)
                    for t in range(T):
                        for k, w in enumerate((w1, w2)):
                            last = Q.tensor_scalar(oh[:, t, k], iota[:], topf[:, t, k:k + 1], w[:, t:t + 1],
                                                   ALU.is_equal, ALU.mult)
                    last.then_inc(oh_s, 1)
                    till(pool, oh_s, nc_)
                    till(pool, yb_s[1], nc_ - 1)
                    till(pool, wT_ready, nc_ - 1)
                    Q.tensor_tensor(wt[:], oh[:, :, 0], oh[:, :, 1], ALU.add).then_inc(wt_s, 1)
                if i is None or 0 <= i + 2 < ROWS:
                    normalise(j, off, off, row + 3)
                if Cc:
                    for t in range(T):
                        till(pool, yc_s[t], nc_)
                        till(pool, ya_s[t], nc_)
                        till(pool, yb_s[t], nc_)
                        last = Q.tensor_tensor(Y[:, t, 0:4 * D], Y[:, t, 0:4 * D], Y[:, t, 4 * D:8 * D], ALU.add)
                    last.then_inc(half_s, 1)
                    till(pool, half_s, nc_)
                    Q.tensor_tensor(Y[:, :, 0:2 * D], Y[:, :, 0:2 * D], Y[:, :, 2 * D:4 * D], ALU.add)\
                        .then_inc(quarter_s, 1)
                    till(pool, quarter_s, nc_)
                    if i is None or i >= 3:
                        pool.wait_ge(stored[1 - off], 16 * (j - 1 + off))
                    Q.tensor_tensor(outb[:, 1 - off], Y[:, :, 0:D], Y[:, :, D:2 * D], ALU.add).then_inc(ysum_s, 1)
                    till(pool, ysum_s, nc_)
                    till(pool, x1w_s, nc_)
                    Q.tensor_tensor(outb[:, 1 - off], outb[:, 1 - off], x1w[:], ALU.add).then_inc(out_s, 1)
            drive2(pool, step2)


_INS = ['x', 'L0_conv_mask', 'L0_conv_gamma', 'L0_conv_beta', 'L0_conv_Wq', 'L0_conv_Wk', 'L0_conv_Wv', 'L0_conv_Wb',
        'L0_conv_Wu', 'L0_conv_bu', 'L0_conv_Wo', 'L0_conv_bo', 'L0_ffn_router_w', 'L0_ffn_router_b',
        'L0_ffn_expert_w', 'L0_ffn_expert_b']


def kernel(**inputs):
    import numpy as _np
    import concourse.bacc as _bacc
    from concourse import mybir as _mybir
    from concourse.bass_utils import run_bass_kernel_spmd as _run

    nc = _bacc.Bacc("TRN2", target_bir_lowering=False, num_devices=1)
    given = {name: _np.ascontiguousarray(inputs[name]) for name in _INS}
    given["eye"] = _np.eye(128, dtype=_np.float32)
    given["iota8"] = _np.tile(_np.arange(8, dtype=_np.float32), (128, 1))
    arrays, args = {}, []
    for name, a in given.items():
        arrays[f"in_{name}_dram"] = a
        args.append(nc.dram_tensor(f"in_{name}_dram", a.shape, _mybir.dt.from_np(a.dtype), kind="ExternalInput").ap())
    args.append(nc.dram_tensor("out_0_dram", given["x"].shape, _mybir.dt.float32, kind="ExternalOutput").ap())
    metaformer_kernel(nc, *args)
    r = _run(nc, [arrays], core_ids=[0])
    return r.results[0]["out_0_dram"]
```

```python
from contextlib import ExitStack

import concourse.bass as bass
from concourse import mybir

ALU = mybir.AluOpType
ACT = mybir.ActivationFunctionType
F32 = mybir.dt.float32
F32R = mybir.dt.float32r
U32 = mybir.dt.uint32


def metaformer_kernel(nc, x, mask, gamma, beta, Wq, Wk, Wv, Wb, Wu, bu, Wo, bo,
                      router_w, router_b, expert_w, expert_b, eye, iota8, out):
    _, ROWS, L, D = x.shape
    HC = Wq.shape[1]
    H = Wb.shape[1]
    C = HC // H
    E = router_w.shape[1]
    P = 128
    T = L // P
    BLK = HC // P
    PAIRS = ROWS // 2
    SCALE = float(C) ** -0.5
    EPS_X, EPS_LN, EPS_T = 1e-6, 1e-5, 1e-5
    EXC = 3
    assert (D, T, BLK, H, C, E) == (128, 2, 2, 4, 64, 8)

    x_pair = x.rearrange("a (m r) (p t) c -> (a m) p r t c", r=2, t=T)
    x_row = x.rearrange("a r (p t) c -> (a r) p t c", t=T)
    out_row = out.rearrange("a r (p t) c -> (a r) p t c", t=T)

    with ExitStack() as ctx:
        def sb(name, shape, dt=F32):
            return ctx.enter_context(nc.sbuf_tensor(name, shape, dt))

        def sem(name):
            return ctx.enter_context(nc.semaphore(name))

        def sems(name, n):
            return [sem(f"{name}{k}") for k in range(n)]

        S = [ctx.enter_context(nc.psum_tensor(f"scores{h}", [P, 512], F32)) for h in range(H)]
        G = [ctx.enter_context(nc.psum_tensor(f"general{k}", [P, 512], F32)) for k in range(3)]
        O = ctx.enter_context(nc.psum_tensor("attended", [P, 512], F32))

        ident = sb("ident", [P, P])
        iota = sb("iota", [P, E])
        gam = sb("gam", [P, 1])
        bet = sb("bet", [P, 1])
        bu_half = sb("bu_half", [P, BLK])
        bo_rows = sb("bo_rows", [P, D])
        rb_rows = sb("rb_rows", [P, E])
        eb = sb("eb", [E, D])
        neg_half = sb("neg_half", [P, 4])
        stage_w = sb("stage_w", [P, 2, E * D])
        wb = sb("wb", [P, H])
        wo = sb("wo", [P, BLK, D])
        wq = [sb("wq_hi", [P, HC], F32R), sb("wq_lo", [P, HC], F32R)]
        wk = [sb("wk_hi", [P, HC], F32R), sb("wk_lo", [P, HC], F32R)]
        wv = [sb("wv_hi", [P, HC], F32R), sb("wv_lo", [P, HC], F32R)]
        wu = [sb("wu_hi", [P, HC], F32R), sb("wu_lo", [P, HC], F32R)]
        EW = E * D + E
        we = [sb("we_hi", [P, EW], F32R), sb("we_lo", [P, EW], F32R)]

        ln_table = sb("ln_table", [P, ROWS, 2 * T])
        biasT = sb("biasT", [P, T, H, ROWS])
        mask_q = sb("mask_q", [P, T, L])
        mask_neg = sb("mask_neg", [P, T, L])
        maskT = sb("maskT", [P, ROWS // 2, 2, T])
        neg_bias = sb("neg_bias", [P, H, T, L])

        x1p = sb("x1p", [P, 4, 2, T, D])
        bn1 = sb("bn1", [P, 2, 4, 6])
        mv1 = sb("mv1", [P, 2, 4, 2])
        ve1 = sb("ve1", [P, 2, 4])
        ln1 = sb("ln1", [P, 2, 2, 2, T])
        xn1 = sb("xn1", [P, 2, 2, T, D])
        xt1 = sb("xt1", [P, 2, 2 * L])

        xin = sb("xin", [P, 2, T, D])
        ln_row = sb("ln_row", [P, 2 * T])
        m_row = sb("m_row", [P, T])
        bom = sb("bom", [P, T, D])
        xb = sb("xb", [P, 2, T, D])
        xn = sb("xn", [P, 2, T, D])
        xt_f = sb("xt_f", [P, L])
        xt = [sb("xt_hi", [P, L], F32R), sb("xt_lo", [P, L], F32R)]
        q2 = [sb("q_hi", [P, BLK * L], F32R), sb("q_lo", [P, BLK * L], F32R)]
        k2 = [sb("k_hi", [P, BLK * L], F32R), sb("k_lo", [P, BLK * L], F32R)]
        v_s = sb("v_s", [P, T, HC])
        th_u = sb("th_u", [P, 2, BLK * L])
        prob = sb("prob", [P, H, T, L])
        neg_max = sb("neg_max", [P, H, T])
        sums = sb("sums", [P, H, T])
        rsum = sb("rsum", [P, H, T])
        pT = sb("pT", [P, H, T * L])
        on = sb("on", [P, T, HC])
        gated = sb("gated", [P, BLK * L])
        x1 = sb("x1", [P, T, D])
        bn2 = sb("bn2", [P, T, 6])
        mv2 = sb("mv2", [P, T, 2])
        ve2 = sb("ve2", [P, T])
        rstd2 = sb("rstd2", [P, T])
        tn = sb("tn", [P, T, D])
        tt = [sb("tt_hi", [P, L], F32R), sb("tt_lo", [P, L], F32R)]
        lg = sb("lg", [P, T, E])
        top = sb("top", [P, T, 8])
        topi = sb("topi", [P, T, 8], U32)
        topf = sb("topf", [P, T, 2])
        gap = sb("gap", [P, T])
        th_g = sb("th_g", [P, T])
        w1 = sb("w1", [P, T])
        w2 = sb("w2", [P, T])
        oh = sb("oh", [P, T, 2, E])
        wt = sb("wt", [P, T, E])
        wT = sb("wT", [E, L])
        Y = sb("Y", [P, T, E * D])
        x1w = sb("x1w", [P, T, D])
        outb = sb("outb", [P, 2, T, D])

        w_in = sem("w_in")
        small_in = sem("small_in")
        mask_in = sem("mask_in")
        consts = sem("consts")
        scaled = sem("scaled")
        hi_made = sem("hi_made")
        staged = sem("staged")
        pair_in = sems("pair_in", 4)
        bn1_s = sem("bn1_s")
        mv1_s = sem("mv1_s")
        ve1_s = sem("ve1_s")
        rs1_s = sem("rs1_s")
        nb1_s = sem("nb1_s")
        tab_s = sem("tab_s")
        xn1_pool = sem("xn1_pool")
        xn1_act = sem("xn1_act")
        xt1_ready = sem("xt1_ready")
        xt1_s = sem("xt1_s")
        pb_ready = sem("pb_ready")
        bt_s = sem("bt_s")
        bt_ready = sem("bt_ready")
        mt_ready = sem("mt_ready")
        mneg_s = sem("mneg_s")
        mt_s = sem("mt_s")
        tables = sem("tables")
        x_in = sems("x_in", 2)
        stored = sems("stored", 2)
        sc_ready = sems("sc_ready", 2)
        wo_ready = sem("wo_ready")
        xt_ready = sem("xt_ready")
        pt_ready = sems("pt_ready", H)
        q_ready = sem("q_ready")
        k_ready = sem("k_ready")
        u_ready = sem("u_ready")
        v_ready = sem("v_ready")
        tt_ready = sem("tt_ready")
        pv_ready = sem("pv_ready")
        ec_ready = sems("ec_ready", T)
        ea_ready = sems("ea_ready", T)
        eb_ready = sems("eb_ready", T)
        wT_ready = sem("wT_ready")
        wb_ready = sem("wb_ready")
        ot_ready = sem("ot_ready")
        exp_s = sems("exp_s", H)
        xtf_s = sem("xtf_s")
        pT_s = sems("pT_s", H)
        qhi_s = sem("qhi_s")
        khi_s = sem("khi_s")
        tthi_s = sem("tthi_s")
        thg_s = sem("thg_s")
        wT_s = sem("wT_s")
        thu_s = sem("thu_s")
        v_s_s = sem("v_s_s")
        lgt_s = sems("lgt_s", 2 * H)
        x1_s = sem("x1_s")
        bn2_s = sem("bn2_s")
        mv2_s = sem("mv2_s")
        ve2_s = sem("ve2_s")
        xthi_s = sem("xthi_s")
        tn_s = sem("tn_s")
        qlo_s = sem("qlo_s")
        klo_s = sem("klo_s")
        ttlo_s = sem("ttlo_s")
        rsum_s = sem("rsum_s")
        lg_s = sem("lg_s")
        top_s = sem("top_s")
        topi_s = sem("topi_s")
        topf_s = sem("topf_s")
        gap_s = sem("gap_s")
        w12_s = sem("w12_s")
        oh_s = sem("oh_s")
        wt_s = sem("wt_s")
        on_s = sem("on_s")
        yc_s = sems("yc_s", T)
        ya_s = sems("ya_s", T)
        yb_s = sems("yb_s", T)
        x1w_s = sem("x1w_s")
        gated_s = sem("gated_s")
        mrow_s = sem("mrow_s")
        bom_s = sem("bom_s")
        xb_s = sem("xb_s")
        lnrow_s = sem("lnrow_s")
        xn_s = sem("xn_s")
        rstd2_s = sem("rstd2_s")
        xtlo_s = sem("xtlo_s")
        half_s = sem("half_s")
        quarter_s = sem("quarter_s")
        ysum_s = sem("ysum_s")
        out_s = sem("out_s")

        def at(j, off):
            return 2 * j + off

        def till(eng, s, n):
            if isinstance(n, int) and n <= 0:
                return
            eng.wait_ge(s, n)

        def till_alone(eng, s, n):
            till(eng, s, n)
            eng.nop(nofuse=True)

        def one(ap, r):
            return ap[r] if isinstance(r, int) else ap[bass.ds(r, 1)].squeeze(0)

        def drive1(eng, step):
            for m in range(4):
                step(0, m, m)
            with eng.Fori(1, PAIRS // 4) as j:
                for off in range(4):
                    step(j, off, None)
            for m in range(PAIRS, PAIRS + 3):
                step(PAIRS // 4, m - PAIRS, m)

        def stages1(m):
            return [m is None or 0 <= m - k < PAIRS for k in range(4)]

        def drive2(eng, step):
            for i in range(-1, 2):
                step(i // 2, i % 2, i)
            with eng.Fori(1, ROWS // 2 - 1) as j:
                step(j, 0, None)
                step(j, 1, None)
            for i in range(ROWS - 2, ROWS + 2):
                step(i // 2, i % 2, i)

        def stages2(i):
            return [i is None or 0 <= i + 1 - k < ROWS for k in range(4)]

        block = ctx.enter_context(nc.Block())

        @block.sync
        def _(sp):
            for k, w in enumerate((Wq, Wk, Wv, Wu)):
                sp.dma_start(stage_w[:, 0, k * HC:(k + 1) * HC], w).then_inc(w_in, 16)
            sp.dma_start(stage_w[:, 1, :].rearrange("p (e c) -> p e c", e=E),
                         expert_w.rearrange("e d c -> d e c")).then_inc(w_in, 16)
            for dst, src in ((ident[:], eye), (iota[:], iota8),
                             (gam[:], gamma.rearrange("(d a) -> d a", a=1)),
                             (bet[:], beta.rearrange("(d a) -> d a", a=1)),
                             (bo_rows[:], bo.partition_broadcast(P)),
                             (rb_rows[:], router_b.partition_broadcast(P)),
                             (eb[:], expert_b), (wb[:], Wb),
                             (wo[:], Wo.rearrange("(b p) d -> p b d", p=P))):
                sp.dma_start(dst, src).then_inc(small_in, 16)
            with nc.allow_non_contiguous_dma(reason="256 biases"):
                sp.dma_start(bu_half[:], bu.rearrange("(b p) -> p b", p=P)).then_inc(small_in, 16)
            sp.dma_start(mask_q[:], mask.rearrange("a (p t) v -> p (a t) v", t=T)).then_inc(mask_in, 16)

            def step1(j, off, m):
                if not stages1(m)[0]:
                    return
                till(sp, xn1_pool, 4 * j + off - 3)
                till(sp, xn1_act, 4 * j + off - 3)
                sp.dma_start(x1p[:, off], one(x_pair, 4 * j + off)).then_inc(pair_in[off], 16)
                if m == 3:
                    sp.wait_ge(staged, 1)
                    sp.dma_start(stage_w[:, 0, 0:E], router_w).then_inc(w_in, 16)
            drive1(sp, step1)

            for r in range(2):
                sp.dma_start(xin[:, r], x_row[r]).then_inc(x_in[r], 16)

            def step2(j, off, i):
                _, b, _, d = stages2(i)
                if b and (i is None or i + 2 < ROWS):
                    till(sp, xb_s, at(j, off) + 1)
                    sp.dma_start(xin[:, off], one(x_row, at(j, off) + 2)).then_inc(x_in[off], 16)
                if d:
                    till(sp, out_s, at(j, off) - 1)
                    sp.dma_start(one(out_row, at(j, off) - 2), outb[:, off]).then_inc(stored[off], 16)
            drive2(sp, step2)
            for k in range(2):
                sp.wait_ge(stored[k], 16 * ROWS // 2)

        @block.tensor
        def _(pe):
            def transpose(dst, src):
                return nc.tensor.transpose(dst, src, ident[:])

            pe.wait_ge(small_in, 16 * 10)

            def step1(j, off, m):
                _, _, s2, s3 = stages1(m)
                par = off % 2
                if s2:
                    n = 4 * j + off - 1
                    till(pe, xn1_pool, n)
                    till(pe, xn1_act, n)
                    till(pe, xt1_s, n - 2)
                    for r in range(2):
                        for t in range(T):
                            mm = transpose(G[par][:, (r * T + t) * P:(r * T + t + 1) * P], xn1[:, par, r, t])
                    mm.then_inc(xt1_ready, 1)
                if s3:
                    n = 4 * j + off - 2
                    till(pe, xt1_s, n)
                    till(pe, bt_s, n - 2)
                    for k in range(2 * T):
                        mm = nc.tensor.matmul(S[1 - par][:, k * H:(k + 1) * H], xt1[:, 1 - par, k * P:(k + 1) * P],
                                              wb[:], start=True, stop=True)
                    mm.then_inc(pb_ready, 1)
            drive1(pe, step1)

            pe.wait_ge(bt_s, PAIRS)
            for h in range(H):
                for a in range(T):
                    for t in range(T):
                        mm = transpose(S[h][:, (a * T + t) * P:(a * T + t + 1) * P], biasT[:, t, h, a::T])
                mm.then_inc(bt_ready, 1)
            pe.wait_ge(mask_in, 16)
            for a in range(2):
                for b in range(T):
                    mm = transpose(O[:, (a * T + b) * P:(a * T + b + 1) * P], mask_q[:, a, b::T])
            mm.then_inc(mt_ready, 1)
            pe.wait_ge(tables, 1)

            def split_product(dst, left, right, lo_left=None, lo_right=None):
                nc.tensor.matmul(dst, left[0], right[0], start=True, stop=False)
                if lo_left:
                    pe.wait_ge(*lo_left)
                nc.tensor.matmul(dst, left[1], right[0], start=False, stop=False)
                if lo_right:
                    pe.wait_ge(*lo_right)
                return nc.tensor.matmul(dst, left[0], right[1], start=False, stop=True)

            def step2(j, off, i):
                A, B, Cc, Dd = stages2(i)
                row = at(j, off)
                na, nb, nc_ = row + 2, row + 1, row

                def scores(pair):
                    if pair == 0:
                        till(pe, qhi_s, nb)
                        till(pe, khi_s, nb)
                        till(pe, qlo_s, nb)
                        till(pe, klo_s, nb)
                    till(pe, ya_s[pair], nb - 2)
                    till(pe, yb_s[pair], nb - 2)
                    if pair == 0:
                        till(pe, pT_s[H - 1], nb - 1)
                    for a in range(T):
                        for kp, qp in ((0, 0), (1, 0), (0, 1)):
                            for e in range(2):
                                rows = slice(e * C, (e + 1) * C)
                                mm = nc.tensor.matmul(
                                    S[2 * pair + e][:, a * L:(a + 1) * L],
                                    k2[kp][rows, pair * L + a * P:pair * L + (a + 1) * P],
                                    q2[qp][rows, pair * L:(pair + 1) * L],
                                    start=(kp, qp) == (0, 0), stop=(kp, qp) == (0, 1))
                    mm.then_inc(sc_ready[pair], 1)

                def probs_transposed(h):
                    till(pe, exp_s[h], nb)
                    for a in range(T):
                        for t in range(T):
                            mm = transpose(S[h][:, t * L + a * P:t * L + (a + 1) * P],
                                           prob[:, h, a, t * P:(t + 1) * P])
                    mm.then_inc(pt_ready[h], 1)

                def attend(h):
                    till(pe, pT_s[h], nb)
                    for a in range(T):
                        for t in range(T):
                            mm = nc.tensor.matmul(O[:, a * HC + h * C:a * HC + (h + 1) * C],
                                                  pT[:, h, t * L + a * P:t * L + (a + 1) * P],
                                                  v_s[:, t, h * C:(h + 1) * C], start=t == 0, stop=t == T - 1)
                    if h == H - 1:
                        mm.then_inc(pv_ready, 1)

                def project_rows(bank, w, ready, lo=None):
                    for b in range(BLK):
                        cols = slice(b * P, (b + 1) * P)
                        mm = split_product(bank[:, b * L:(b + 1) * L], [w[0][:, cols], w[1][:, cols]],
                                           [xt[0][:], xt[1][:]], lo_right=lo if b == 0 else None)
                    mm.then_inc(ready, 1)

                def experts(bank, t, first, width, ready):
                    cols = slice(first * D, first * D + width)
                    toks = slice(t * P, (t + 1) * P)
                    split_product(bank[:, 0:width], [tt[0][:, toks], tt[1][:, toks]],
                                  [we[0][:, cols], we[1][:, cols]]).then_inc(ready, 1)

                if B:
                    scores(0)
                if A:
                    till(pe, xn_s, na)
                    till(pe, yc_s[1], nc_ - 1)
                    if not Cc:
                        till(pe, xtf_s, na - 1)
                    for t in range(T):
                        mm = transpose(G[2][:, t * P:(t + 1) * P], xn[:, 1 - off, t])
                    mm.then_inc(xt_ready, 1)
                if Cc:
                    till(pe, gated_s, nc_)
                    till(pe, x1w_s, nc_ - 1)
                    if B and (i is None or i >= 1):
                        till(pe, v_s_s, nb)
                    for a in range(T):
                        for b in range(BLK):
                            mm = nc.tensor.matmul(G[0][:, a * D:(a + 1) * D],
                                                  gated[:, b * L + a * P:b * L + (a + 1) * P], wo[:, b, :],
                                                  start=b == 0, stop=b == BLK - 1)
                    mm.then_inc(wo_ready, 1)
                if B:
                    scores(1)
                if A:
                    till(pe, gated_s, nc_)
                    till(pe, xthi_s, na)
                    project_rows(G[1], wq, q_ready, lo=(xtlo_s, na))
                if B:
                    probs_transposed(0)
                    probs_transposed(1)
                if A:
                    if Cc:
                        till(pe, x1_s, nc_)
                    else:
                        till(pe, v_s_s, nb)
                    project_rows(G[0], wk, k_ready)
                if B:
                    till(pe, on_s, nb - 1)
                    till(pe, thu_s, nb)
                    till(pe, v_s_s, nb)
                    attend(0)
                if Cc:
                    till(pe, tn_s, nc_)
                    if A:
                        till(pe, xtf_s, na)
                    for t in range(T):
                        mm = transpose(G[2][:, t * P:(t + 1) * P], tn[:, t])
                    mm.then_inc(tt_ready, 1)
                if B:
                    attend(1)
                    probs_transposed(2)
                    probs_transposed(3)
                if Cc:
                    till(pe, tthi_s, nc_)
                    till(pe, ttlo_s, nc_)
                    if A:
                        till(pe, qlo_s, na)
                    experts(G[1], 0, 2 * EXC, 2 * D + E, ec_ready[0])
                    experts(G[2], 1, 2 * EXC, 2 * D + E, ec_ready[1])
                if B:
                    attend(2)
                    attend(3)
                if A:
                    till(pe, klo_s, na)
                    for t in range(T):
                        toks = slice(t * P, (t + 1) * P)
                        mm = split_product(G[0][:, t * HC:(t + 1) * HC], [xt[0][:, toks], xt[1][:, toks]],
                                           [wv[0][:], wv[1][:]])
                    mm.then_inc(v_ready, 1)
                    till(pe, on_s, nb)
                    project_rows(O, wu, u_ready)
                if Cc:
                    till(pe, wt_s, nc_)
                    if A:
                        till(pe, v_s_s, na)
                    else:
                        till(pe, x1_s, nc_)
                    for t in range(T):
                        mm = transpose(G[0][0:E, t * P:(t + 1) * P], wt[:, t])
                    mm.then_inc(wT_ready, 1)
                    for t in range(T):
                        for s in range(2):
                            if B:
                                till(pe, pT_s[2 * t + s], nb)
                            experts(S[2 * t + s], t, EXC * s, EXC * D, (ea_ready, eb_ready)[s][t])
                        if t == 0:
                            till(pe, wT_s, nc_)
                            for a in range(T):
                                mm = nc.tensor.matmul(G[0][:, a * D:(a + 1) * D], wT[:, a * P:(a + 1) * P], eb[:],
                                                      start=True, stop=True)
                            mm.then_inc(wb_ready, 1)
                if B:
                    till(pe, on_s, nb)
                    if Cc:
                        till(pe, yc_s[0], nc_)
                    elif A:
                        till(pe, qlo_s, na)
                    for b in range(BLK):
                        for a in range(T):
                            mm = transpose(G[1][:, b * L + a * P:b * L + (a + 1) * P], on[:, a, b * P:(b + 1) * P])
                    mm.then_inc(ot_ready, 1)
            drive2(pe, step2)

        @block.scalar
        def _(act):
            def step1(j, off, m):
                _, s1, s2, _ = stages1(m)
                par = off % 2
                if s1:
                    n = 4 * j + off
                    till(act, nb1_s, n)
                    till(act, xt1_ready, n - 2)
                    for t in range(T):
                        last = nc.scalar.activation(xn1[:, 1 - par, 1, t], x1p[:, (off + 3) % 4, 1, t], ACT.Identity,
                                                    bias=ln1[:, 1 - par, 1, 1, t:t + 1],
                                                    scale=ln1[:, 1 - par, 1, 0, t:t + 1])
                    last.then_inc(xn1_act, 1)
                if s2:
                    n = 4 * j + off - 1
                    till(act, xt1_ready, n)
                    till(act, pb_ready, n - 2)
                    nc.scalar.activation(xt1[:, par], G[par][:], ACT.Identity, bias=bet[:], scale=gam[:])\
                        .then_inc(xt1_s, 1)
            act.wait_ge(small_in, 16 * 10)
            drive1(act, step1)
            act.wait_ge(tables, 1)

            def step2(j, off, i):
                A, B, Cc, Dd = stages2(i)
                row = at(j, off)
                na, nb, nc_ = row + 2, row + 1, row

                def exps(h, a):
                    till(act, lgt_s[2 * h + a], nb)
                    if h == 0 and a == 0:
                        till(act, rsum_s, nb - 1)
                    ex = nc.scalar.activation(prob[:, h, a], prob[:, h, a], ACT.Exp, scale=-1.0,
                                              bias=neg_max[:, h, a:a + 1], accum_out=sums[:, h, a:a + 1])
                    if a == T - 1:
                        ex.then_inc(exp_s[h], 1)

                def probs_out(h):
                    till(act, pt_ready[h], nb)
                    till(act, pv_ready, nb - 1)
                    nc.scalar.copy(pT[:, h], S[h][:]).then_inc(pT_s[h], 1)

                if A:
                    till(act, xt_ready, na)
                    till(act, xtlo_s, na - 1)
                    nc.scalar.activation(xt_f[:], G[2][:, 0:L], ACT.Identity, bias=bet[:], scale=gam[:])\
                        .then_inc(xtf_s, 1)
                if B:
                    exps(0, 0)
                    exps(1, 0)
                    exps(0, 1)
                    exps(1, 1)
                if A:
                    till(act, q_ready, na)
                    till(act, sc_ready[1], nb)
                    nc.scalar.copy(q2[0][:], G[1][:]).then_inc(qhi_s, 1)
                if B:
                    probs_out(0)
                    exps(2, 0)
                    probs_out(1)
                    exps(3, 0)
                if A:
                    till(act, k_ready, na)
                    nc.scalar.copy(k2[0][:], G[0][:]).then_inc(khi_s, 1)
                if B:
                    exps(2, 1)
                if Cc:
                    till(act, tt_ready, nc_)
                    till(act, eb_ready[1], nc_ - 1)
                    nc.scalar.copy(tt[0][:], G[2][:, 0:L]).then_inc(tthi_s, 1)
                if B:
                    exps(3, 1)
                    probs_out(2)
                    probs_out(3)
                if Cc:
                    till(act, gap_s, nc_)
                    nc.scalar.activation(th_g[:], gap[:], ACT.Tanh, scale=0.5).then_inc(thg_s, 1)
                if A:
                    till(act, v_ready, na)
                    till(act, pv_ready, nb)
                    nc.scalar.copy(v_s[:].rearrange("p t c -> p (t c)"), G[0][:]).then_inc(v_s_s, 1)
                    till(act, u_ready, na)
                    till(act, gated_s, nc_)
                    for b in range(BLK):
                        last = nc.scalar.activation(th_u[:, 1 - off, b * L:(b + 1) * L], O[:, b * L:(b + 1) * L],
                                                    ACT.Tanh, bias=bu_half[:, b:b + 1], scale=0.5)
                    last.then_inc(thu_s, 1)
                if Cc:
                    till(act, wT_ready, nc_)
                    till(act, wb_ready, nc_ - 1)
                    nc.scalar.copy(wT[:], G[0][0:E, 0:L]).then_inc(wT_s, 1)
            drive2(act, step2)

        @block.vector
        def _(dve):
            V = nc.vector
            V.memset(neg_half[:], -0.5).then_inc(consts, 1)
            dve.wait_ge(small_in, 16 * 10)
            V.tensor_scalar(bu_half[:], bu_half[:], 0.5, None, ALU.mult).then_inc(scaled, 1)
            V.tensor_scalar(wo[:], wo[:], 0.5, None, ALU.mult).then_inc(scaled, 1)
            dve.wait_ge(w_in, 16 * 5)
            V.tensor_scalar(stage_w[:, 0, 0:HC], stage_w[:, 0, 0:HC], -SCALE, None, ALU.mult).then_inc(scaled, 1)
            dve.wait_ge(scaled, 3)
            for k, w in enumerate((wq, wk, wv, wu)):
                V.tensor_copy(w[0][:], stage_w[:, 0, k * HC:(k + 1) * HC]).then_inc(hi_made, 1)
            V.tensor_copy(we[0][:, 0:E * D], stage_w[:, 1, :]).then_inc(hi_made, 1)
            dve.wait_ge(hi_made, 5)
            for k, w in enumerate((wq, wk, wv, wu)):
                lo = V.tensor_tensor(w[1][:], stage_w[:, 0, k * HC:(k + 1) * HC], w[0][:].bitcast(F32), ALU.subtract)
            lo.then_inc(staged, 1)
            V.tensor_tensor(we[1][:, 0:E * D], stage_w[:, 1, :], we[0][:, 0:E * D].bitcast(F32),
                            ALU.subtract).then_inc(staged, 1)

            def step1(j, off, m):
                s0, s1, _, s3 = stages1(m)
                par = off % 2
                n = 4 * j + off + 1
                if s0:
                    till(dve, pair_in[off], (j + 1) * 16)
                    till(dve, mv1_s, n - 2)
                    for k in range(4):
                        last = V.bn_stats(bn1[:, par, k], x1p[:, off, k // 2, k % 2])
                    last.then_inc(bn1_s, 1)
                if s1:
                    till(dve, rs1_s, n - 1)
                    V.scalar_tensor_tensor(ln1[:, 1 - par, :, 1, :],
                                           mv1[:, 1 - par, :, 0].rearrange("p (r t) -> p r t", r=2),
                                           -1.0, ln1[:, 1 - par, :, 0, :], ALU.mult, ALU.mult).then_inc(nb1_s, 1)
                if s0:
                    till(dve, nb1_s, n - 2)
                    till_alone(dve, bn1_s, n)
                    for k in range(4):
                        last = V.bn_aggr(mv1[:, par, k], bn1[:, par, k])
                    last.then_inc(mv1_s, 1)
                if s1:
                    till(dve, nb1_s, n - 1)
                    V.tensor_copy(ln_table[:, bass.ds(2 * (n - 2), 2), :],
                                  ln1[:, 1 - par].rearrange("p r k t -> p r (k t)")).then_inc(tab_s, 1)
                if s3:
                    till(dve, pb_ready, n - 3)
                    V.tensor_copy(biasT[:, :, :, bass.ds(2 * (n - 4), 2)],
                                  S[1 - par][:, 0:2 * T * H].rearrange("p (r t h) -> p t h r", r=2, t=T))\
                        .then_inc(bt_s, 1)
                if s0:
                    till(dve, mv1_s, n)
                    till(dve, rs1_s, n - 2)
                    V.tensor_scalar(ve1[:, par], mv1[:, par, :, 1], 1.0 + EPS_LN, EPS_X * EPS_LN,
                                    ALU.mult, ALU.add).then_inc(ve1_s, 1)
                if m == 3:
                    dve.wait_ge(w_in, 16 * 6)
                    V.tensor_copy(we[0][:, E * D:EW], stage_w[:, 0, 0:E]).then_inc(hi_made, 1)
                    dve.wait_ge(hi_made, 6)
                    V.tensor_tensor(we[1][:, E * D:EW], stage_w[:, 0, 0:E], we[0][:, E * D:EW].bitcast(F32),
                                    ALU.subtract).then_inc(staged, 1)
            drive1(dve, step1)

            dve.wait_ge(mask_in, 16)
            V.tensor_scalar(mask_neg[:].rearrange("p a (t v) -> p a t v", t=T),
                            mask_q[:].rearrange("p a (v t) -> p a t v", t=T),
                            -1.0, -1.0e9, ALU.add, ALU.mult).then_inc(mneg_s, 1)
            dve.wait_ge(mneg_s, 1)
            for h in range(H):
                dve.wait_ge(bt_ready, h + 1)
                V.tensor_tensor(neg_bias[:, h].rearrange("p a v -> p (a v)"),
                                mask_neg[:].rearrange("p a v -> p (a v)"), S[h][:], ALU.subtract)\
                    .then_inc(mt_s, 1)
            dve.wait_ge(mt_ready, 1)
            for b in range(T):
                V.tensor_copy(maskT[:, :, :, b],
                              O[:].rearrange("p (a b s) -> p b s a", a=2, b=T)[:, b]).then_inc(mt_s, 1)
            dve.wait_ge(mt_s, H + T)
            dve.wait_ge(staged, 3)
            dve.wait_ge(scaled, 3)
            V.memset(neg_half[:], -0.5).then_inc(tables, 1)

            def step2(j, off, i):
                A, B, Cc, Dd = stages2(i)
                row = at(j, off)
                na, nb, nc_ = row + 2, row + 1, row

                def logits(h, a):
                    till(dve, sc_ready[h // 2], nb)
                    till_alone(dve, pt_ready[h], nb - 1)
                    V.tensor_tensor_reduce(prob[:, h, a], S[h][:, a * L:(a + 1) * L], neg_bias[:, h, a], 1.0, 0.0,
                                           ALU.add, ALU.min, neg_max[:, h, a:a + 1]).then_inc(lgt_s[2 * h + a], 1)

                if B:
                    logits(0, 0)
                    logits(1, 0)
                if A:
                    till(dve, xtf_s, na)
                    till(dve, u_ready, na - 1)
                    V.tensor_copy(xt[0][:], xt_f[:]).then_inc(xthi_s, 1)
                if B:
                    logits(0, 1)
                    logits(1, 1)
                if Cc:
                    till(dve, wo_ready, nc_)
                    till(dve, xb_s, nc_)
                    till(dve, x1w_s, nc_ - 1)
                    mrow = maskT[:].rearrange("p s a t -> p (s a) t")
                    for t in range(T):
                        last = V.scalar_tensor_tensor(x1[:, t], G[0][:, t * D:(t + 1) * D],
                                                      mrow[:, bass.ds(row - 1, 1), t], xb[:, 1 - off, t],
                                                      ALU.mult, ALU.add)
                    last.then_inc(x1_s, 1)
                if B:
                    logits(2, 0)
                if Cc:
                    till(dve, x1_s, nc_)
                    for t in range(T):
                        last = V.bn_stats(bn2[:, t], x1[:, t])
                    last.then_inc(bn2_s, 1)
                if B:
                    logits(3, 0)
                if Cc:
                    till_alone(dve, bn2_s, nc_)
                    for t in range(T):
                        last = V.bn_aggr(mv2[:, t], bn2[:, t])
                    last.then_inc(mv2_s, 1)
                if B:
                    logits(2, 1)
                if Cc:
                    till(dve, mv2_s, nc_)
                    V.tensor_scalar(ve2[:], mv2[:, :, 1], EPS_T, None, ALU.add).then_inc(ve2_s, 1)
                if B:
                    logits(3, 1)
                if A:
                    till(dve, qhi_s, na)
                    V.tensor_tensor(q2[1][:], G[1][:], q2[0][:].bitcast(F32), ALU.subtract).then_inc(qlo_s, 1)
                if Cc:
                    till(dve, rstd2_s, nc_)
                    till(dve, tt_ready, nc_ - 1)
                    for t in range(T):
                        last = V.tensor_scalar(tn[:, t], x1[:, t], mv2[:, t, 0:1], rstd2[:, t:t + 1],
                                               ALU.subtract, ALU.mult)
                    last.then_inc(tn_s, 1)
                if A:
                    till(dve, khi_s, na)
                    V.tensor_tensor(k2[1][:], G[0][:], k2[0][:].bitcast(F32), ALU.subtract).then_inc(klo_s, 1)
                if Cc:
                    till(dve, tthi_s, nc_)
                    V.tensor_tensor(tt[1][:], G[2][:, 0:L], tt[0][:].bitcast(F32), ALU.subtract).then_inc(ttlo_s, 1)
                if B:
                    till(dve, exp_s[H - 1], nb)
                    till(dve, on_s, nb - 1)
                    V.reciprocal(rsum[:], sums[:]).then_inc(rsum_s, 1)
                if Cc:
                    for t in range(T):
                        till(dve, ec_ready[t], nc_)
                        last = V.tensor_tensor(lg[:, t], G[1 + t][:, 2 * D:2 * D + E], rb_rows[:], ALU.add)
                    last.then_inc(lg_s, 1)
                    till_alone(dve, lg_s, nc_)
                    for t in range(T):
                        last = V.max(top[:, t], lg[:, t])
                    last.then_inc(top_s, 1)
                    till_alone(dve, top_s, nc_)
                    till_alone(dve, thg_s, nc_ - 1)
                    V.tensor_tensor(gap[:], top[:, :, 0], top[:, :, 1], ALU.subtract).then_inc(gap_s, 1)
                    for t in range(T):
                        last = V.max_index(topi[:, t], top[:, t], lg[:, t])
                    last.then_inc(topi_s, 1)
                    till(dve, topi_s, nc_)
                    V.tensor_copy(topf[:], topi[:, :, 0:2]).then_inc(topf_s, 1)
                if B:
                    till(dve, pv_ready, nb)
                    till(dve, rsum_s, nb)
                    till(dve, ot_ready, nb - 1)
                    V.tensor_tensor(on[:].rearrange("p t (h c) -> p t h c", h=H),
                                    O[:].rearrange("p (t h c) -> p t h c", t=T, h=H),
                                    rsum[:].rearrange("p h t -> p t h").unsqueeze(3).to_broadcast([P, T, H, C]),
                                    ALU.mult).then_inc(on_s, 1)
                if Cc:
                    till(dve, thg_s, nc_)
                    V.tensor_scalar(w1[:], th_g[:], 0.5, 0.5, ALU.mult, ALU.add)
                    V.tensor_scalar(w2[:], th_g[:], -0.5, 0.5, ALU.mult, ALU.add).then_inc(w12_s, 1)
                    till(dve, w12_s, nc_)
                    till(dve, topf_s, nc_)
                    for t in range(T):
                        for k, w in enumerate((w1, w2)):
                            last = V.tensor_scalar(oh[:, t, k], iota[:], topf[:, t, k:k + 1], w[:, t:t + 1],
                                                   ALU.is_equal, ALU.mult)
                    last.then_inc(oh_s, 1)
                    till(dve, oh_s, nc_)
                    till(dve, wT_ready, nc_ - 1)
                    V.tensor_tensor(wt[:], oh[:, :, 0], oh[:, :, 1], ALU.add).then_inc(wt_s, 1)

                    def weigh(bank, t, first, n, ready, done):
                        till(dve, ready, nc_)
                        V.tensor_tensor(Y[:, t, first * D:(first + n) * D].rearrange("p (e c) -> p e c", e=n),
                                        bank[:, 0:n * D].rearrange("p (e c) -> p e c", e=n),
                                        wt[:, t, first:first + n].unsqueeze(2).to_broadcast([P, n, D]),
                                        ALU.mult).then_inc(done, 1)
                    till(dve, wt_s, nc_)
                    till(dve, ysum_s, nc_ - 1)
                    for t in range(T):
                        weigh(G[1 + t], t, 2 * EXC, 2, ec_ready[t], yc_s[t])
                    for t in range(T):
                        weigh(S[2 * t], t, 0, EXC, ea_ready[t], ya_s[t])
                        weigh(S[2 * t + 1], t, EXC, EXC, eb_ready[t], yb_s[t])
                        if t == 0:
                            till(dve, wb_ready, nc_)
                            till(dve, out_s, nc_ - 1)
                            V.tensor_tensor(x1w[:].rearrange("p t c -> p (t c)"), G[0][:, 0:T * D],
                                            x1[:].rearrange("p t c -> p (t c)"), ALU.add).then_inc(x1w_s, 1)
                if B:
                    till(dve, ot_ready, nb)
                    till(dve, thu_s, nb)
                    till(dve, wo_ready, nb - 1)
                    V.scalar_tensor_tensor(gated[:], th_u[:, off], 1.0, G[1][:], ALU.add, ALU.mult)\
                        .then_inc(gated_s, 1)
            drive2(dve, step2)

        @block.gpsimd
        def _(pool):
            Q = nc.gpsimd
            pool.wait_ge(consts, 1)

            def step1(j, off, m):
                s0, s1, _, _ = stages1(m)
                par = off % 2
                n = 4 * j + off + 1
                if s1:
                    till(pool, nb1_s, n - 1)
                    till_alone(pool, xt1_ready, n - 3)
                    for t in range(T):
                        last = Q.tensor_scalar(xn1[:, 1 - par, 0, t], x1p[:, (off + 3) % 4, 0, t],
                                               ln1[:, 1 - par, 0, 0, t:t + 1], ln1[:, 1 - par, 0, 1, t:t + 1],
                                               ALU.mult, ALU.add)
                    last.then_inc(xn1_pool, 1)
                if s0:
                    till(pool, ve1_s, n)
                    till(pool, xn1_act, n - 2)
                    till(pool, xn1_pool, n - 2)
                    till(pool, tab_s, n - 2)
                    Q.tensor_tensor(ln1[:, par, :, 0, :], ve1[:, par].rearrange("p (r t) -> p r t", r=2),
                                    neg_half[:].rearrange("p (r t) -> p r t", r=2), ALU.pow).then_inc(rs1_s, 1)
            drive1(pool, step1)
            pool.wait_ge(tables, 1)
            pool.wait_ge(tab_s, PAIRS)

            def normalise(j, off, par, n):
                row = n - 1
                till(pool, x_in[par], 16 * (j + (off + 2) // 2) + 16)
                till_alone(pool, xn_s, n - 1)
                src = ln_table[:, row, :] if isinstance(row, int) else ln_table[:, bass.ds(row, 1), :].squeeze(1)
                Q.tensor_copy(ln_row[:], src).then_inc(lnrow_s, 1)
                till(pool, lnrow_s, n)
                till_alone(pool, xt_ready, n - 2)
                for t in range(T):
                    last = Q.tensor_scalar(xn[:, par, t], xin[:, par, t], ln_row[:, t:t + 1],
                                           ln_row[:, T + t:T + t + 1], ALU.mult, ALU.add)
                last.then_inc(xn_s, 1)

            def step2(j, off, i):
                A, B, Cc, Dd = stages2(i)
                row = at(j, off)
                na, nb, nc_ = row + 2, row + 1, row
                if i == -1:
                    normalise(-1, 0, 0, 1)
                if A:
                    till(pool, xthi_s, na)
                    Q.tensor_tensor(xt[1][:], xt_f[:], xt[0][:].bitcast(F32), ALU.subtract).then_inc(xtlo_s, 1)
                if Cc:
                    till(pool, ve2_s, nc_)
                    till(pool, tn_s, nc_ - 1)
                    Q.tensor_tensor(rstd2[:], ve2[:], neg_half[:, 0:T], ALU.pow).then_inc(rstd2_s, 1)
                if Dd:
                    nd = nc_ - 1
                    for t in range(T):
                        till(pool, yc_s[t], nd)
                        till(pool, ya_s[t], nd)
                        till(pool, yb_s[t], nd)
                        last = Q.tensor_tensor(Y[:, t, 0:4 * D], Y[:, t, 0:4 * D], Y[:, t, 4 * D:8 * D], ALU.add)
                    last.then_inc(half_s, 1)
                    till(pool, half_s, nd)
                    Q.tensor_tensor(Y[:, :, 0:2 * D], Y[:, :, 0:2 * D], Y[:, :, 2 * D:4 * D], ALU.add)\
                        .then_inc(quarter_s, 1)
                    till(pool, quarter_s, nd)
                    if i is None or i >= 4:
                        pool.wait_ge(stored[off], 16 * (j - 1))
                    Q.tensor_tensor(outb[:, off], Y[:, :, 0:D], Y[:, :, D:2 * D], ALU.add).then_inc(ysum_s, 1)
                    till(pool, ysum_s, nd)
                    till(pool, x1w_s, nd)
                    Q.tensor_tensor(outb[:, off], outb[:, off], x1w[:], ALU.add).then_inc(out_s, 1)
                if B:
                    till_alone(pool, bom_s, nb - 1)
                    mrow = maskT[:].rearrange("p s a t -> p (s a) t")
                    src = mrow[:, row, :] if isinstance(row, int) else mrow[:, bass.ds(row, 1), :].squeeze(1)
                    Q.tensor_copy(m_row[:], src).then_inc(mrow_s, 1)
                    till(pool, mrow_s, nb)
                    till_alone(pool, xb_s, nb - 1)
                    for t in range(T):
                        last = Q.tensor_scalar(bom[:, t], bo_rows[:], m_row[:, t:t + 1], 1.0, ALU.mult, ALU.mult)
                    last.then_inc(bom_s, 1)
                    till(pool, bom_s, nb)
                    till(pool, x1_s, nb - 2)
                    Q.tensor_tensor(xb[:, off], xin[:, off], bom[:], ALU.add).then_inc(xb_s, 1)
                if i is None or 0 <= i + 2 < ROWS:
                    normalise(j, off, off, row + 3)
            drive2(pool, step2)


_INS = ['x', 'L0_conv_mask', 'L0_conv_gamma', 'L0_conv_beta', 'L0_conv_Wq', 'L0_conv_Wk', 'L0_conv_Wv', 'L0_conv_Wb',
        'L0_conv_Wu', 'L0_conv_bu', 'L0_conv_Wo', 'L0_conv_bo', 'L0_ffn_router_w', 'L0_ffn_router_b',
        'L0_ffn_expert_w', 'L0_ffn_expert_b']


def kernel(**inputs):
    import numpy as _np
    import concourse.bacc as _bacc
    from concourse import mybir as _mybir
    from concourse.bass_utils import run_bass_kernel_spmd as _run

    nc = _bacc.Bacc("TRN2", target_bir_lowering=False, num_devices=1)
    given = {name: _np.ascontiguousarray(inputs[name]) for name in _INS}
    given["eye"] = _np.eye(128, dtype=_np.float32)
    given["iota8"] = _np.tile(_np.arange(8, dtype=_np.float32), (128, 1))
    arrays, args = {}, []
    for name, a in given.items():
        arrays[f"in_{name}_dram"] = a
        args.append(nc.dram_tensor(f"in_{name}_dram", a.shape, _mybir.dt.from_np(a.dtype), kind="ExternalInput").ap())
    args.append(nc.dram_tensor("out_0_dram", given["x"].shape, _mybir.dt.float32, kind="ExternalOutput").ap())
    metaformer_kernel(nc, *args)
    r = _run(nc, [arrays], core_ids=[0])
    return r.results[0]["out_0_dram"]
```

```python
from contextlib import ExitStack

import concourse.bass as bass
from concourse import mybir

ALU = mybir.AluOpType
ACT = mybir.ActivationFunctionType
F32 = mybir.dt.float32
F32R = mybir.dt.float32r
U32 = mybir.dt.uint32


def metaformer_kernel(nc, x, mask, gamma, beta, Wq, Wk, Wv, Wb, Wu, bu, Wo, bo,
                      router_w, router_b, expert_w, expert_b, eye, iota8, out):
    _, ROWS, L, D = x.shape
    HC = Wq.shape[1]
    H = Wb.shape[1]
    C = HC // H
    E = router_w.shape[1]
    P = 128
    T = L // P
    BLK = HC // P
    PAIRS = 4
    GR = 2 * PAIRS
    TILES = GR * T
    GROUPS = ROWS // GR
    DVE_TILES, POOL_TILES, ACT_TILES = range(2), range(2, 8), range(8, TILES)
    SCALE = float(C) ** -0.5
    EPS_X, EPS_LN, EPS_T = 1e-6, 1e-5, 1e-5
    EXC = 3
    assert (D, T, BLK, H, C, E) == (128, 2, 2, 4, 64, 8)

    x_group = x.rearrange("a (m r) (p t) c -> (a m) p r t c", r=GR, t=T)
    x_row = x.rearrange("a r (p t) c -> (a r) p t c", t=T)
    out_row = out.rearrange("a r (p t) c -> (a r) p t c", t=T)

    with ExitStack() as ctx:
        def sb(name, shape, dt=F32):
            return ctx.enter_context(nc.sbuf_tensor(name, shape, dt))

        def sem(name):
            return ctx.enter_context(nc.semaphore(name))

        def sems(name, n):
            return [sem(f"{name}{k}") for k in range(n)]

        bias_rows = nc.dram_tensor("pair_bias", (ROWS // 2, H, T * L), F32, kind="Internal").ap()

        B = [ctx.enter_context(nc.psum_tensor(f"bank{k}", [P, 512], F32)) for k in range(8)]
        SC_BANK = (B[6], B[0], B[7], B[4])
        PT_BANK = (B[3], B[1], B[6], B[2])
        XT_BANK = B[5]
        Q_BANK = B[0]
        K_BANK = B[2]
        U_BANK = B[3]
        V_BANK = B[5]
        AT_BANK = B[3]
        WO_BANK = B[5]
        TT_BANK = B[3]
        WT_BANK = B[3]
        WB_BANK = B[7]
        EC_BANK = (B[1], B[6])
        EA_BANK = (B[7], B[2])
        EB_BANK = (B[1], B[4])

        ident = sb("ident", [P, P])
        iota = sb("iota", [P, E])
        gam = sb("gam", [P, 1])
        bet = sb("bet", [P, 1])
        bu_half = sb("bu_half", [P, BLK])
        bo_rows = sb("bo_rows", [P, D])
        rb_rows = sb("rb_rows", [P, E])
        eb2 = sb("eb2", [T * E, T * D])
        neg_half = sb("neg_half", [P, TILES])
        WB_COLS = 32
        wb = sb("wb", [P, WB_COLS])
        wo = sb("wo", [P, BLK, D])
        wq = [sb("wq_hi", [P, HC], F32R), sb("wq_lo", [P, HC], F32R)]
        wk = [sb("wk_hi", [P, HC], F32R), sb("wk_lo", [P, HC], F32R)]
        wv = [sb("wv_hi", [P, HC], F32R), sb("wv_lo", [P, HC], F32R)]
        wu = [sb("wu_hi", [P, HC], F32R), sb("wu_lo", [P, HC], F32R)]
        EW = E * D + E
        stage_w = sb("stage_w", [P, 4 * HC])
        stage_e = sb("stage_e", [P, EW])
        we = [sb("we_hi", [P, EW], F32R), sb("we_lo", [P, EW], F32R)]

        ln_table = sb("ln_table", [P, ROWS, 2 * T])
        mask_q = sb("mask_q", [P, T, L])
        mask_neg = sb("mask_neg", [P, T, L])
        maskT = sb("maskT", [P, ROWS // 2, 2, T])
        neg_bias = sb("neg_bias", [P, H, T, L])

        xg = sb("xg", [P, 4, GR, T, D])
        bn1 = sb("bn1", [P, 2, TILES, 6])
        mv1 = sb("mv1", [P, 2, TILES, 2])
        ve1 = sb("ve1", [P, 2, TILES])
        ln1 = sb("ln1", [P, 2, GR, 2, T])
        xt1 = sb("xt1", [P, PAIRS, 2 * L])
        pb = sb("pb", [P, 2, 2 * L])

        xin = sb("xin", [P, 4, T, D])
        ln_row = sb("ln_row", [P, 2 * T])
        m_row = sb("m_row", [P, T])
        bom = sb("bom", [P, T, D])
        xb = sb("xb", [P, 2, T, D])
        xn = sb("xn", [P, 2, T, D])
        xt_f = sb("xt_f", [P, L])
        xt = [sb("xt_hi", [P, L], F32R), sb("xt_lo", [P, L], F32R)]
        q2 = [sb("q_hi", [P, BLK * L], F32R), sb("q_lo", [P, BLK * L], F32R)]
        k2 = [sb("k_hi", [P, BLK * L], F32R), sb("k_lo", [P, BLK * L], F32R)]
        v_s = sb("v_s", [P, T, HC])
        th_u = sb("th_u", [P, 2, BLK * L])
        prob = sb("prob", [P, H, T, L])
        neg_max = sb("neg_max", [P, H, T])
        sums = sb("sums", [P, H, T])
        rsum = sb("rsum", [P, H, T])
        pT = sb("pT", [P, H, T * L])
        gated = sb("gated", [P, BLK * L])
        x1 = sb("x1", [P, T, D])
        bn2 = sb("bn2", [P, T, 6])
        mv2 = sb("mv2", [P, T, 2])
        ve2 = sb("ve2", [P, T])
        rstd2 = sb("rstd2", [P, T])
        nmr = sb("nmr", [P, T])
        tn = sb("tn", [P, T, D])
        tt = [sb("tt_hi", [P, L], F32R), sb("tt_lo", [P, L], F32R)]
        lg = sb("lg", [P, T, E])
        top = sb("top", [P, T, 8])
        topi = sb("topi", [P, T, 8], U32)
        topf = sb("topf", [P, T, 2])
        gap = sb("gap", [P, T])
        th_g = sb("th_g", [P, T])
        w12 = sb("w12", [P, T, 2])
        oh = sb("oh", [P, T, 2, E])
        ohw = sb("ohw", [P, T, 2, E])
        wt = sb("wt", [P, T, E])
        wT = sb("wT", [T * E, P])
        Y = sb("Y", [P, 2, T, E * D])
        x1w = sb("x1w", [P, T, D])
        outb = sb("outb", [P, 2, T, D])

        w_in = sem("w_in")
        first_in = sem("first_in")
        rest_in = sem("rest_in")
        mask_in = sem("mask_in")
        consts = sem("consts")
        scaled = sem("scaled")
        hi_made = sem("hi_made")
        lo_made = sem("lo_made")
        bias_in = sem("bias_in")
        group_in = sems("group_in", 4)
        bn1_s = sem("bn1_s")
        mv1_s = sem("mv1_s")
        ve1_s = sem("ve1_s")
        rs1_s = sem("rs1_s")
        nb1_s = sem("nb1_s")
        tab_s = sem("tab_s")
        xn1_dve = sem("xn1_dve")
        xn1_pool = sem("xn1_pool")
        xn1_act = sem("xn1_act")
        xt1_ready = sem("xt1_ready")
        xt1_s = sem("xt1_s")
        pb_ready = sem("pb_ready")
        pb_s = sem("pb_s")
        pb_moved = sems("pb_moved", 2)
        mt_ready = sem("mt_ready")
        mneg_s = sem("mneg_s")
        mt_s = sem("mt_s")
        nb_s = sem("nb_s")
        x_in = sems("x_in", 4)
        stored = sems("stored", 2)
        sc_ready = sems("sc_ready", 2)
        wo_ready = sem("wo_ready")
        xt_ready = sem("xt_ready")
        pt_ready = sems("pt_ready", H)
        q_ready = sem("q_ready")
        k_ready = sems("k_ready", BLK)
        u_ready = sem("u_ready")
        v_ready = sem("v_ready")
        tt_ready = sem("tt_ready")
        pv_ready = sems("pv_ready", BLK)
        ec_ready = sems("ec_ready", T)
        ea_ready = sems("ea_ready", T)
        eb_ready = sems("eb_ready", T)
        wT_ready = sem("wT_ready")
        wb_ready = sem("wb_ready")
        exp_s = sems("exp_s", 2 * H)
        xtf_s = sem("xtf_s")
        pT_s = sems("pT_s", H)
        qhi_s = sem("qhi_s")
        khi_s = sem("khi_s")
        tthi_s = sem("tthi_s")
        thg_s = sem("thg_s")
        wT_s = sem("wT_s")
        thu_s = sem("thu_s")
        v_s_s = sem("v_s_s")
        lgt_s = sems("lgt_s", 2 * H)
        x1_s = sem("x1_s")
        bn2_s = sem("bn2_s")
        mv2_s = sem("mv2_s")
        ve2_s = sem("ve2_s")
        nmr_s = sem("nmr_s")
        xthi_s = sem("xthi_s")
        tn_s = sem("tn_s")
        qlo_s = sem("qlo_s")
        klo_s = sem("klo_s")
        ttlo_s = sem("ttlo_s")
        rsum_s = sems("rsum_s", H)
        lg_s = sem("lg_s")
        top_s = sem("top_s")
        topi_s = sem("topi_s")
        topf_s = sem("topf_s")
        gap_s = sem("gap_s")
        w12_s = sem("w12_s")
        oh_s = sem("oh_s")
        ohw_s = sem("ohw_s")
        wt_s = sem("wt_s")
        prob_s = sems("prob_s", H)
        yc_s = sems("yc_s", T)
        ya_s = sems("ya_s", T)
        yb_s = sems("yb_s", T)
        x1w_s = sem("x1w_s")
        gated_s = sem("gated_s")
        mrow_s = sem("mrow_s")
        bom_s = sem("bom_s")
        xb_s = sem("xb_s")
        lnrow_s = sem("lnrow_s")
        xn_s = sem("xn_s")
        rstd2_s = sem("rstd2_s")
        xtlo_s = sem("xtlo_s")
        half_s = sems("half_s", T)
        quarter_s = sem("quarter_s")
        ysum_s = sem("ysum_s")
        out_s = sem("out_s")

        def till(eng, s, n):
            if isinstance(n, int) and n <= 0:
                return
            eng.wait_ge(s, n)

        def xt_used(eng, n):
            for s in (q_ready, *k_ready, u_ready, v_ready):
                till(eng, s, n)

        def till_alone(eng, s, n):
            till(eng, s, n)
            eng.nop(nofuse=True)

        def one(ap, r):
            return ap[r] if isinstance(r, int) else ap[bass.ds(r, 1)].squeeze(0)

        def drive1(eng, step, peeled=0):
            for m in range(8):
                step(m // 4, m % 4, m)
            with eng.Fori(2, GROUPS // 4 - peeled) as j:
                for off in range(4):
                    step(j, off, None)
            for m in range(GROUPS - 4 * peeled, GROUPS + 4):
                step(m // 4, m % 4, m)

        def stages1(j, off, m):
            return ([m is None or 0 <= m - k < GROUPS for k in range(5)],
                    [4 * j + off + 1 - k for k in range(5)])

        def group_tile(k, off, lag):
            row, t = k // T, k % T
            par = (off - lag) % 2
            return (xg[:, (off - lag) % 4, row, t], ln1[:, par, row, 0, t:t + 1], ln1[:, par, row, 1, t:t + 1])

        LAG = 4
        FIRST_EXPERTS = 3

        def drive2(eng, step, peeled=0):
            for i in range(8):
                step(i // 4, i % 4, i)
            with eng.Fori(2, ROWS // 4 - peeled) as j:
                for off in range(4):
                    step(j, off, None)
            for i in range(ROWS - 4 * peeled, ROWS + LAG):
                step(i // 4, i % 4, i)

        def stages2(j, off, i):
            return ([i is None or 0 <= i - k < ROWS for k in range(LAG + 1)],
                    [4 * j + off + 1 - k for k in range(LAG + 1)])

        block = ctx.enter_context(nc.Block())

        @block.sync
        def _(sp):
            sp.dma_start(xg[:, 0], x_group[0]).then_inc(group_in[0], 16)
            sp.wait_ge(consts, 3)
            for dst, src in ((ident[:], eye), (wb[:, 0:H], Wb),
                             (gam[:], gamma.rearrange("(d a) -> d a", a=1)),
                             (bet[:], beta.rearrange("(d a) -> d a", a=1))):
                sp.dma_start(dst, src).then_inc(first_in, 16)

            def rest():
                for k, w in enumerate((Wq, Wk, Wv, Wu)):
                    sp.dma_start(stage_w[:, k * HC:(k + 1) * HC], w).then_inc(w_in, 16)
                sp.dma_start(stage_e[:, 0:E * D].rearrange("p (e c) -> p e c", e=E),
                             expert_w.rearrange("e d c -> d e c")).then_inc(w_in, 16)
                sp.dma_start(stage_e[:, E * D:EW], router_w).then_inc(w_in, 16)
                sp.dma_start(wo[:], Wo.rearrange("(b p) d -> p b d", p=P)).then_inc(w_in, 16)
                with nc.allow_non_contiguous_dma(reason="256 biases"):
                    sp.dma_start(bu_half[:], bu.rearrange("(b p) -> p b", p=P)).then_inc(w_in, 16)
                for dst, src in ((iota[:], iota8),
                                 (bo_rows[:], bo.partition_broadcast(P)),
                                 (rb_rows[:], router_b.partition_broadcast(P)),
                                 (eb2[0:E, 0:D], expert_b),
                                 (eb2[E:2 * E, D:2 * D], expert_b)):
                    sp.dma_start(dst, src).then_inc(rest_in, 16)
                for r in range(4):
                    sp.dma_start(xin[:, r], x_row[r]).then_inc(x_in[r], 16)
                sp.dma_start(mask_q[:], mask.rearrange("a (p t) v -> p (a t) v", t=T)).then_inc(mask_in, 16)

            EARLY = GROUPS - 4

            def bias_of_groups(first, last):
                for par in range(2):
                    sp.wait_ge(pb_moved[par], 16 * PAIRS * last // 2)
                rows = slice(first * PAIRS, last * PAIRS)
                sp.dma_start(neg_bias[rows].rearrange("p h a l -> p h (a l)"), bias_rows[rows])\
                    .then_inc(bias_in, 16)

            def step1(j, off, m):
                on, n = stages1(j, off, m)
                if on[0] and (m is None or m + 1 < GROUPS):
                    till(sp, xt1_ready, PAIRS * (n[0] - 3))
                    sp.dma_start(xg[:, (off + 1) % 4], one(x_group, n[0])).then_inc(group_in[(off + 1) % 4], 16)
                if m == 2:
                    rest()
                if m == GROUPS + 1:
                    bias_of_groups(0, EARLY)
                if on[4]:
                    till(sp, pb_s, n[4])
                    for q in range(PAIRS):
                        sp.dma_start(one(bias_rows, PAIRS * (n[4] - 1) + q),
                                     pb[q * WB_COLS:q * WB_COLS + H, off % 2]).then_inc(pb_moved[off % 2], 16)
            drive1(sp, step1, peeled=1)

            bias_of_groups(EARLY, GROUPS)

            def step2(j, off, i):
                on, n = stages2(j, off, i)
                if on[2] and (i is None or i + 2 < ROWS):
                    till(sp, xn_s, n[2])
                    till(sp, xb_s, n[2])
                    sp.dma_start(xin[:, (off - 2) % 4], one(x_row, n[2] + 3))\
                        .then_inc(x_in[(off - 2) % 4], 16)
                if on[4]:
                    till(sp, out_s, n[4])
                    sp.dma_start(one(out_row, n[4] - 1), outb[:, (off - 4) % 2])\
                        .then_inc(stored[(off - 4) % 2], 16)
            drive2(sp, step2, peeled=1)
            for k in range(2):
                sp.wait_ge(stored[k], 16 * ROWS // 2)

        @block.tensor
        def _(pe):
            def transpose(dst, src):
                return nc.tensor.transpose(dst, src, ident[:])

            pe.wait_ge(first_in, 16 * 4)

            def step1(j, off, m):
                on, n = stages1(j, off, m)
                if on[2]:
                    for done in (xn1_dve, xn1_pool, xn1_act):
                        till(pe, done, n[2])
                    for q in range(PAIRS):
                        till(pe, xt1_s, PAIRS * n[2] - 2 * PAIRS + 1 + q)
                        for r in range(2):
                            for t in range(T):
                                mm = transpose(B[4 + q][:, (r * T + t) * P:(r * T + t + 1) * P],
                                               xg[:, (off - 2) % 4, 2 * q + r, t])
                        mm.then_inc(xt1_ready, 1)
                    till(pe, pb_s, n[2] - 2)
                    for q in range(PAIRS):
                        till(pe, xt1_s, PAIRS * n[2] - PAIRS + 1 + q)
                        nc.tensor.matmul(B[off % 2][q * WB_COLS:(q + 1) * WB_COLS, :], wb[:], xt1[:, q],
                                         start=True, stop=True).then_inc(pb_ready, 1)
                if m == 3:
                    pe.wait_ge(mask_in, 16)
                    for a in range(2):
                        for b in range(T):
                            mm = transpose(B[2][:, (a * T + b) * P:(a * T + b + 1) * P], mask_q[:, a, b::T])
                    mm.then_inc(mt_ready, 1)
            drive1(pe, step1)

            pe.wait_ge(pb_s, GROUPS)
            pe.wait_ge(mt_s, T)
            pe.wait_ge(lo_made, 4)
            pe.wait_ge(rest_in, 16 * 5)

            def split_product(dst, left, right):
                for k, (le, ri) in enumerate(((0, 0), (1, 0), (0, 1))):
                    mm = nc.tensor.matmul(dst, left[le], right[ri], start=k == 0, stop=k == 2)
                return mm

            def step2(j, off, i):
                on, n = stages2(j, off, i)

                def turn(latest, *reads):
                    if i is None:
                        for s, rows in reads[:latest]:
                            till(pe, s, rows)
                    else:
                        for s, rows in reads:
                            till(pe, s, min(rows, ROWS))

                def scores(pair, n):
                    till(pe, qlo_s, n)
                    till(pe, klo_s, n)
                    for a in range(T):
                        for kp, qp in ((0, 0), (1, 0), (0, 1)):
                            for e in range(2):
                                part = slice(e * C, (e + 1) * C)
                                mm = nc.tensor.matmul(
                                    SC_BANK[2 * pair + e][:, a * L:(a + 1) * L],
                                    k2[kp][part, pair * L + a * P:pair * L + (a + 1) * P],
                                    q2[qp][part, pair * L:(pair + 1) * L],
                                    start=(kp, qp) == (0, 0), stop=(kp, qp) == (0, 1))
                    mm.then_inc(sc_ready[pair], 1)

                def probs_transposed(h, n):
                    till(pe, prob_s[h], n)
                    for a in range(T):
                        for t in range(T):
                            mm = transpose(PT_BANK[h][:, t * L + a * P:t * L + (a + 1) * P],
                                           prob[:, h, a, t * P:(t + 1) * P])
                    mm.then_inc(pt_ready[h], 1)

                def attend(pair, n):
                    till(pe, v_s_s, n)
                    till(pe, pT_s[2 * pair], n)
                    till(pe, pT_s[2 * pair + 1], n)
                    for t in range(T):
                        for e in range(2):
                            h = 2 * pair + e
                            mm = nc.tensor.matmul(AT_BANK[e * C:(e + 1) * C, pair * L:(pair + 1) * L],
                                                  v_s[:, t, h * C:(h + 1) * C], pT[:, h, t * L:(t + 1) * L],
                                                  start=t == 0, stop=t == T - 1)
                    mm.then_inc(pv_ready[pair], 1)

                def project_rows(bank, w, blocks, ready, n):
                    till(pe, xthi_s, n)
                    till(pe, xtlo_s, n)
                    for b in blocks:
                        cols = slice(b * P, (b + 1) * P)
                        mm = split_product(bank[:, b * L:(b + 1) * L], [w[0][:, cols], w[1][:, cols]],
                                           [xt[0][:], xt[1][:]])
                    mm.then_inc(ready, 1)

                def experts(bank, t, first, width, ready, n):
                    till(pe, ttlo_s, n)
                    cols = slice(first * D, first * D + width)
                    toks = slice(t * P, (t + 1) * P)
                    split_product(bank[:, 0:width], [tt[0][:, toks], tt[1][:, toks]],
                                  [we[0][:, cols], we[1][:, cols]]).then_inc(ready, 1)

                if i == FIRST_EXPERTS:
                    pe.wait_ge(lo_made, 5)
                if on[1]:
                    project_rows(K_BANK, wk, range(1, 2), k_ready[1], n[1])
                    turn(2, (lgt_s[2], n[1] - 1), (lgt_s[3], n[1] - 1), (qlo_s, n[1] - 1))
                    project_rows(Q_BANK, wq, range(BLK), q_ready, n[1])
                if on[4]:
                    turn(2, (lgt_s[6], n[1] - 1), (lgt_s[7], n[1] - 1), (yb_s[1], n[4] - 1))
                    experts(EB_BANK[1], 1, EXC, EXC * D, eb_ready[1], n[4])
                    turn(1, (gated_s, n[2] - 1), (ttlo_s, n[3] - 1), (pT_s[0], n[2] - 1), (thu_s, n[1] - 1),
                            (wT_s, n[4] - 1))
                    till(pe, wt_s, n[4])
                    transpose(WT_BANK[0:T * E, 0:P], wt[:].rearrange("p t e -> p (t e)")).then_inc(wT_ready, 1)
                if on[3]:
                    turn(1, (v_s_s, n[1] - 1), (xtf_s, n[0] - 1), (x1_s, n[3] - 1))
                    till(pe, gated_s, n[3])
                    for a in range(T):
                        for b in range(BLK):
                            mm = nc.tensor.matmul(WO_BANK[:, a * D:(a + 1) * D],
                                                  gated[:, b * L + a * P:b * L + (a + 1) * P], wo[:, b, :],
                                                  start=b == 0, stop=b == BLK - 1)
                    mm.then_inc(wo_ready, 1)
                if on[4]:
                    turn(2, (lgt_s[4], n[1] - 1), (lgt_s[5], n[1] - 1), (ya_s[0], n[4] - 1), (x1w_s, n[4] - 1))
                    till(pe, wT_s, n[4])
                    nc.tensor.matmul(WB_BANK[:, 0:T * D], wT[:], eb2[:], start=True, stop=True).then_inc(wb_ready, 1)
                if on[1]:
                    turn(1, (wT_s, n[4]), (gated_s, n[2] - 1), (ttlo_s, n[3] - 1), (pT_s[0], n[2] - 1),
                            (thu_s, n[1] - 1))
                    project_rows(U_BANK, wu, range(BLK), u_ready, n[1])
                if on[4]:
                    turn(1, (klo_s, n[0] - 1), (pT_s[3], n[2] - 1), (ya_s[1], n[4] - 1))
                    experts(EA_BANK[1], 1, 0, EXC * D, ea_ready[1], n[4])
                    turn(1, (x1w_s, n[4]), (lgt_s[4], n[1] - 1), (lgt_s[5], n[1] - 1), (ya_s[0], n[4] - 1))
                    experts(EA_BANK[0], 0, 0, EXC * D, ea_ready[0], n[4])
                if on[0]:
                    turn(1, (x1_s, n[3]), (v_s_s, n[1] - 1), (xtf_s, n[0] - 1))
                    till(pe, xn_s, n[0])
                    for t in range(T):
                        mm = transpose(XT_BANK[:, t * P:(t + 1) * P], xn[:, off % 2, t])
                    mm.then_inc(xt_ready, 1)
                if on[2]:
                    turn(1, (yc_s[1], n[3] - 1), (lgt_s[0], n[1] - 1), (lgt_s[1], n[1] - 1), (pT_s[2], n[2] - 1))
                    probs_transposed(2, n[2])
                    turn(1, (thu_s, n[1]), (wT_s, n[4]), (gated_s, n[2] - 1), (ttlo_s, n[3] - 1),
                            (pT_s[0], n[2] - 1))
                    probs_transposed(0, n[2])
                if on[4]:
                    turn(1, (yc_s[0], n[3] - 1), (pT_s[1], n[2] - 1), (yb_s[0], n[4] - 1))
                    experts(EB_BANK[0], 0, EXC, EXC * D, eb_ready[0], n[4])
                if on[1]:
                    turn(1, (xtf_s, n[0]), (x1_s, n[3]), (v_s_s, n[1] - 1))
                    till(pe, xthi_s, n[1])
                    till(pe, xtlo_s, n[1])
                    for t in range(T):
                        toks = slice(t * P, (t + 1) * P)
                        mm = split_product(V_BANK[:, t * HC:(t + 1) * HC], [xt[0][:, toks], xt[1][:, toks]],
                                           [wv[0][:], wv[1][:]])
                    mm.then_inc(v_ready, 1)
                    turn(1, (pT_s[2], n[2]), (yc_s[1], n[3] - 1), (lgt_s[0], n[1] - 1), (lgt_s[1], n[1] - 1))
                    turn(1, (qlo_s, n[1]), (lgt_s[2], n[1] - 1), (lgt_s[3], n[1] - 1))
                    scores(0, n[1])
                if on[2]:
                    turn(1, (ya_s[1], n[4]), (klo_s, n[0] - 1), (pT_s[3], n[2] - 1))
                    probs_transposed(3, n[2])
                    turn(1, (yb_s[0], n[4]), (yc_s[0], n[3] - 1), (pT_s[1], n[2] - 1))
                    probs_transposed(1, n[2])
                if on[3]:
                    turn(1, (pT_s[0], n[2]), (thu_s, n[1]), (wT_s, n[4]), (gated_s, n[2] - 1), (ttlo_s, n[3] - 1))
                    till(pe, tn_s, n[3])
                    for t in range(T):
                        mm = transpose(TT_BANK[:, t * P:(t + 1) * P], tn[:, t])
                    mm.then_inc(tt_ready, 1)
                if on[1]:
                    turn(1, (ya_s[0], n[4]), (x1w_s, n[4]), (lgt_s[4], n[1] - 1), (lgt_s[5], n[1] - 1))
                    turn(1, (yb_s[1], n[4]), (lgt_s[6], n[1] - 1), (lgt_s[7], n[1] - 1))
                    scores(1, n[1])
                if on[3]:
                    turn(1, (pT_s[1], n[2]), (yb_s[0], n[4]), (yc_s[0], n[3] - 1))
                    experts(EC_BANK[0], 0, 2 * EXC, 2 * D + E, ec_ready[0], n[3])
                    turn(2, (lgt_s[0], n[1]), (lgt_s[1], n[1]), (pT_s[2], n[2]), (yc_s[1], n[3] - 1))
                    experts(EC_BANK[1], 1, 2 * EXC, 2 * D + E, ec_ready[1], n[3])
                if on[2]:
                    turn(1, (ttlo_s, n[3]), (pT_s[0], n[2]), (thu_s, n[1]), (wT_s, n[4]), (gated_s, n[2] - 1))
                    attend(1, n[2])
                    attend(0, n[2])
                if on[0]:
                    turn(1, (pT_s[3], n[2]), (ya_s[1], n[4]), (klo_s, n[0] - 1))
                    project_rows(K_BANK, wk, range(0, 1), k_ready[0], n[0])
            drive2(pe, step2)

        @block.scalar
        def _(act):
            def step1(j, off, m):
                on, n = stages1(j, off, m)
                half = len(ACT_TILES) // 2
                for first, tiles in ((0, ACT_TILES[:half]), (PAIRS // 2, ACT_TILES[half:])):
                    if on[1]:
                        till(act, nb1_s, n[1])
                        for k in tiles:
                            x_t, rstd, shift = group_tile(k, off, 1)
                            last = nc.scalar.activation(x_t, x_t, ACT.Identity, bias=shift, scale=rstd)
                        if first:
                            last.then_inc(xn1_act, 1)
                    if on[2]:
                        for q in range(first, first + PAIRS // 2):
                            till(act, xt1_ready, PAIRS * n[2] - PAIRS + 1 + q)
                            till(act, pb_ready, PAIRS * n[2] - 2 * PAIRS + 1 + q)
                            nc.scalar.activation(xt1[:, q], B[4 + q][:], ACT.Identity, bias=bet[:], scale=gam[:])\
                                .then_inc(xt1_s, 1)
            act.wait_ge(first_in, 16 * 4)
            drive1(act, step1)
            act.wait_ge(scaled, 3)

            def step2(j, off, i):
                on, n = stages2(j, off, i)

                def exps(h, a, n):
                    till(act, lgt_s[2 * h + a], n)
                    till(act, rsum_s[h], n - 1)
                    nc.scalar.activation(prob[:, h, a], prob[:, h, a], ACT.Exp, scale=-1.0,
                                         bias=neg_max[:, h, a:a + 1], accum_out=sums[:, h, a:a + 1])\
                        .then_inc(exp_s[2 * h + a], 1)

                def norm_probs(h, n):
                    till(act, rsum_s[h], n)
                    for a in range(T):
                        last = nc.scalar.activation(prob[:, h, a], prob[:, h, a], ACT.Copy,
                                                    scale=rsum[:, h, a:a + 1])
                    last.then_inc(prob_s[h], 1)

                def probs_out(h, n):
                    till(act, pt_ready[h], n)
                    till(act, pv_ready[h // 2], n - 1)
                    nc.scalar.copy(pT[:, h], PT_BANK[h][:]).then_inc(pT_s[h], 1)

                if on[1]:
                    till(act, k_ready[0], n[1])
                    till(act, k_ready[1], n[1])
                    till(act, sc_ready[0], n[1] - 1)
                    till(act, sc_ready[1], n[1] - 1)
                    nc.scalar.copy(k2[0][:], K_BANK[:]).then_inc(khi_s, 1)
                    till(act, q_ready, n[1])
                    till(act, sc_ready[0], n[1] - 1)
                    till(act, sc_ready[1], n[1] - 1)
                    nc.scalar.copy(q2[0][:], Q_BANK[:]).then_inc(qhi_s, 1)
                if on[4]:
                    till(act, wT_ready, n[4])
                    till(act, wb_ready, n[4] - 1)
                    nc.scalar.copy(wT[:], WT_BANK[0:T * E, 0:P]).then_inc(wT_s, 1)
                if on[2]:
                    exps(1, 1, n[2])
                    norm_probs(0, n[2])
                if on[1]:
                    till(act, u_ready, n[1])
                    till(act, gated_s, n[1] - 2)
                    for b in range(BLK):
                        cols = slice(b * L, (b + 1) * L)
                        last = nc.scalar.activation(th_u[:, (off - 1) % 2, cols], U_BANK[:, cols], ACT.Tanh,
                                                    bias=bu_half[:, b:b + 1], scale=0.5)
                    last.then_inc(thu_s, 1)
                if on[2]:
                    exps(3, 1, n[2])
                if on[0]:
                    till(act, xt_ready, n[0])
                    till(act, xthi_s, n[0] - 1)
                    till(act, xtlo_s, n[0] - 1)
                    nc.scalar.activation(xt_f[:], XT_BANK[:, 0:L], ACT.Identity, bias=bet[:], scale=gam[:])\
                        .then_inc(xtf_s, 1)
                if on[2]:
                    probs_out(2, n[2])
                    norm_probs(3, n[2])
                    norm_probs(1, n[2])
                    probs_out(0, n[2])
                    probs_out(3, n[2])
                if on[3]:
                    till(act, tt_ready, n[3])
                    for t in range(T):
                        till(act, ec_ready[t], n[3] - 1)
                        till(act, ea_ready[t], n[3] - 1)
                        till(act, eb_ready[t], n[3] - 1)
                    nc.scalar.copy(tt[0][:], TT_BANK[:, 0:L]).then_inc(tthi_s, 1)
                if on[2]:
                    probs_out(1, n[2])
                if on[1]:
                    exps(0, 1, n[1])
                    exps(0, 0, n[1])
                    exps(1, 0, n[1])
                    exps(2, 0, n[1])
                    exps(2, 1, n[1])
                if on[3]:
                    till(act, gap_s, n[3])
                    till(act, w12_s, n[3] - 1)
                    nc.scalar.activation(th_g[:], gap[:], ACT.Tanh, scale=0.5).then_inc(thg_s, 1)
                if on[1]:
                    exps(3, 0, n[1])
                    till(act, v_ready, n[1])
                    for pair in range(BLK):
                        till(act, pv_ready[pair], n[1] - 1)
                    nc.scalar.copy(v_s[:].rearrange("p t c -> p (t c)"), V_BANK[:]).then_inc(v_s_s, 1)
            drive2(act, step2)

        @block.vector
        def _(dve):
            V = nc.vector
            V.memset(neg_half[:], -0.5).then_inc(consts, 1)
            V.memset(wb[:], 0.0).then_inc(consts, 1)
            V.memset(eb2[:], 0.0).then_inc(consts, 1)

            def split_weights():
                dve.wait_ge(w_in, 16 * 8)
                V.tensor_scalar(bu_half[:], bu_half[:], 0.5, None, ALU.mult).then_inc(scaled, 1)
                V.tensor_scalar(wo[:], wo[:], 0.5, None, ALU.mult).then_inc(scaled, 1)
                V.tensor_scalar(stage_w[:, 0:HC], stage_w[:, 0:HC], -SCALE, None, ALU.mult).then_inc(scaled, 1)
                dve.wait_ge(scaled, 3)
                split([(w, stage_w[:, k * HC:(k + 1) * HC]) for k, w in enumerate((wq, wk, wv, wu))], 4)

            def split(parts, total):
                for w, full in parts:
                    V.tensor_copy(w[0][:], full).then_inc(hi_made, 1)
                dve.wait_ge(hi_made, total)
                for w, full in parts:
                    V.tensor_tensor(w[1][:], full, w[0][:].bitcast(F32), ALU.subtract).then_inc(lo_made, 1)

            def mask_logits():
                dve.wait_ge(mask_in, 16)
                V.tensor_scalar(mask_neg[:].rearrange("p a (t v) -> p a t v", t=T),
                                mask_q[:].rearrange("p a (v t) -> p a t v", t=T),
                                -1.0, -1.0e9, ALU.add, ALU.mult).then_inc(mneg_s, 1)

            def mask_columns():
                dve.wait_ge(mt_ready, 1)
                for b in range(T):
                    V.tensor_copy(maskT[:, :, :, b],
                                  B[2][:].rearrange("p (a b s) -> p b s a", a=2, b=T)[:, b]).then_inc(mt_s, 1)

            def bias_table():
                dve.wait_ge(mneg_s, 1)
                dve.wait_ge(bias_in, 16 * 2)
                for h in range(H):
                    V.tensor_tensor(neg_bias[:, h], mask_neg[:], neg_bias[:, h], ALU.subtract).then_inc(nb_s, 1)
                dve.wait_ge(nb_s, H)

            def step1(j, off, m):
                on, n = stages1(j, off, m)
                par = off % 2
                if on[0]:
                    till(dve, group_in[off], (j + 1) * 16)
                    for k in range(TILES):
                        last = V.bn_stats(bn1[:, par, k], xg[:, off, k // T, k % T])
                    last.then_inc(bn1_s, 1)
                if on[1]:
                    till(dve, rs1_s, n[1])
                    V.scalar_tensor_tensor(ln1[:, 1 - par, :, 1, :],
                                           mv1[:, 1 - par, :, 0].rearrange("p (r t) -> p r t", r=GR),
                                           -1.0, ln1[:, 1 - par, :, 0, :], ALU.mult, ALU.mult).then_inc(nb1_s, 1)
                if on[0]:
                    till_alone(dve, bn1_s, n[0])
                    for k in range(TILES):
                        last = V.bn_aggr(mv1[:, par, k], bn1[:, par, k])
                    last.then_inc(mv1_s, 1)
                if on[1]:
                    till(dve, nb1_s, n[1])
                    for k in DVE_TILES:
                        x_t, rstd, shift = group_tile(k, off, 1)
                        last = V.tensor_scalar(x_t, x_t, rstd, shift, ALU.mult, ALU.add)
                    last.then_inc(xn1_dve, 1)
                if on[0]:
                    till(dve, mv1_s, n[0])
                    till(dve, rs1_s, n[0] - 2)
                    V.tensor_scalar(ve1[:, par], mv1[:, par, :, 1], 1.0 + EPS_LN, EPS_X * EPS_LN,
                                    ALU.mult, ALU.add).then_inc(ve1_s, 1)
                if on[1]:
                    V.tensor_copy(ln_table[:, bass.ds(GR * (n[1] - 1), GR), :],
                                  ln1[:, 1 - par].rearrange("p r k t -> p r (k t)")).then_inc(tab_s, 1)
                if on[3]:
                    till(dve, pb_ready, PAIRS * n[3])
                    till(dve, pb_moved[1 - par], 16 * PAIRS * (2 * j + (off - 3) // 2))
                    V.tensor_copy(pb[:, 1 - par], B[1 - par][:]).then_inc(pb_s, 1)
                if m == 3:
                    split_weights()
                    mask_logits()
                if m == 5:
                    mask_columns()
            drive1(dve, step1)

            dve.wait_ge(rest_in, 16 * 5)

            mask_rows = maskT[:].rearrange("p s a t -> p (s a) t")

            def step2(j, off, i):
                on, n = stages2(j, off, i)

                def logits(h, a, n):
                    till(dve, sc_ready[h // 2], n)
                    till_alone(dve, pt_ready[h], n - 1)
                    V.tensor_tensor_reduce(prob[:, h, a], SC_BANK[h][:, a * L:(a + 1) * L], neg_bias[:, h, a],
                                           1.0, 0.0, ALU.add, ALU.min,
                                           neg_max[:, h, a:a + 1]).then_inc(lgt_s[2 * h + a], 1)

                def norm_sums(h, n):
                    for a in range(T):
                        till(dve, exp_s[2 * h + a], n)
                    till(dve, prob_s[h], n - 1)
                    V.reciprocal(rsum[:, h], sums[:, h]).then_inc(rsum_s[h], 1)

                def norm_probs(h, n):
                    till(dve, rsum_s[h], n)
                    for a in range(T):
                        last = V.tensor_scalar(prob[:, h, a], prob[:, h, a], rsum[:, h, a:a + 1], None, ALU.mult)
                    last.then_inc(prob_s[h], 1)

                def weigh(bank, buf, t, first, num, ready, done, n):
                    till(dve, wt_s, n)
                    till(dve, ready, n)
                    till(dve, ysum_s, n - 2)
                    V.tensor_tensor(Y[:, buf, t, first * D:(first + num) * D].rearrange("p (e c) -> p e c", e=num),
                                    bank[:, 0:num * D].rearrange("p (e c) -> p e c", e=num),
                                    wt[:, t, first:first + num].unsqueeze(2).to_broadcast([P, num, D]),
                                    ALU.mult).then_inc(done, 1)

                if i == 1:
                    bias_table()
                if i == FIRST_EXPERTS - 1:
                    split([(we, stage_e[:])], 5)
                if on[2]:
                    norm_probs(2, n[2])
                if on[1]:
                    till(dve, khi_s, n[1])
                    V.tensor_tensor(k2[1][:], K_BANK[:], k2[0][:].bitcast(F32), ALU.subtract).then_inc(klo_s, 1)
                if on[4]:
                    weigh(EC_BANK[1], (off - 4) % 2, 1, 2 * EXC, 2, ec_ready[1], yc_s[1], n[4])
                    till(dve, wb_ready, n[4])
                    till(dve, x1_s, n[4])
                    till(dve, out_s, n[4] - 1)
                    V.tensor_tensor(x1w[:].rearrange("p t c -> p (t c)"), WB_BANK[:, 0:T * D],
                                    x1[:].rearrange("p t c -> p (t c)"), ALU.add).then_inc(x1w_s, 1)
                if on[3]:
                    till(dve, wo_ready, n[3])
                    till(dve, xb_s, n[3])
                    till(dve, x1w_s, n[3] - 1)
                    till(dve, tn_s, n[3] - 1)
                    for t in range(T):
                        last = V.scalar_tensor_tensor(x1[:, t], WO_BANK[:, t * D:(t + 1) * D],
                                                      mask_rows[:, bass.ds(n[3] - 1, 1), t], xb[:, (off - 3) % 2, t],
                                                      ALU.mult, ALU.add)
                    last.then_inc(x1_s, 1)
                if on[4]:
                    weigh(EC_BANK[0], (off - 4) % 2, 0, 2 * EXC, 2, ec_ready[0], yc_s[0], n[4])
                if on[3]:
                    till(dve, x1_s, n[3])
                    for t in range(T):
                        last = V.bn_stats(bn2[:, t], x1[:, t])
                    last.then_inc(bn2_s, 1)
                if on[1]:
                    till(dve, qhi_s, n[1])
                    V.tensor_tensor(q2[1][:], Q_BANK[:], q2[0][:].bitcast(F32), ALU.subtract).then_inc(qlo_s, 1)
                if on[3]:
                    till(dve, bn2_s, n[3])
                    till_alone(dve, tn_s, n[3] - 1)
                    for t in range(T):
                        last = V.bn_aggr(mv2[:, t], bn2[:, t])
                    last.then_inc(mv2_s, 1)
                if on[2]:
                    norm_sums(1, n[2])
                    norm_sums(3, n[2])
                if on[3]:
                    till(dve, mv2_s, n[3])
                    till(dve, rstd2_s, n[3] - 1)
                    V.tensor_scalar(ve2[:], mv2[:, :, 1], EPS_T, None, ALU.add).then_inc(ve2_s, 1)
                if on[4]:
                    weigh(EA_BANK[1], (off - 4) % 2, 1, 0, EXC, ea_ready[1], ya_s[1], n[4])
                    weigh(EB_BANK[0], (off - 4) % 2, 0, EXC, EXC, eb_ready[0], yb_s[0], n[4])
                if on[3]:
                    till(dve, rstd2_s, n[3])
                    till(dve, tn_s, n[3] - 1)
                    V.scalar_tensor_tensor(nmr[:], mv2[:, :, 0], -1.0, rstd2[:], ALU.mult, ALU.mult).then_inc(nmr_s, 1)
                if on[4]:
                    weigh(EA_BANK[0], (off - 4) % 2, 0, 0, EXC, ea_ready[0], ya_s[0], n[4])
                    weigh(EB_BANK[1], (off - 4) % 2, 1, EXC, EXC, eb_ready[1], yb_s[1], n[4])
                if on[0]:
                    till(dve, xtf_s, n[0])
                    xt_used(dve, n[0] - 1)
                    V.tensor_copy(xt[0][:], xt_f[:]).then_inc(xthi_s, 1)
                if on[1]:
                    logits(0, 1, n[1])
                    logits(0, 0, n[1])
                    logits(1, 0, n[1])
                if on[3]:
                    till(dve, tthi_s, n[3])
                    V.tensor_tensor(tt[1][:], TT_BANK[:, 0:L], tt[0][:].bitcast(F32), ALU.subtract).then_inc(ttlo_s, 1)
                if on[1]:
                    logits(1, 1, n[1])
                    logits(2, 0, n[1])
                    logits(2, 1, n[1])
                if on[3]:
                    for t in range(T):
                        till(dve, ec_ready[t], n[3])
                        last = V.tensor_tensor(lg[:, t], EC_BANK[t][:, 2 * D:2 * D + E], rb_rows[:], ALU.add)
                    last.then_inc(lg_s, 1)
                if on[1]:
                    norm_sums(0, n[1])
                if on[3]:
                    till_alone(dve, lg_s, n[3])
                    for t in range(T):
                        last = V.max(top[:, t], lg[:, t])
                    last.then_inc(top_s, 1)
                if on[1]:
                    logits(3, 0, n[1])
                if on[3]:
                    till_alone(dve, top_s, n[3])
                    for t in range(T):
                        last = V.max_index(topi[:, t], top[:, t], lg[:, t])
                    last.then_inc(topi_s, 1)
                    till(dve, top_s, n[3])
                    till(dve, thg_s, n[3] - 1)
                    V.tensor_tensor(gap[:], top[:, :, 0], top[:, :, 1], ALU.subtract).then_inc(gap_s, 1)
                if on[1]:
                    logits(3, 1, n[1])
                if on[3]:
                    till(dve, topi_s, n[3])
                    V.tensor_copy(topf[:], topi[:, :, 0:2]).then_inc(topf_s, 1)
                    till(dve, thg_s, n[3])
                    V.tensor_scalar(w12[:, :, 0], th_g[:], 0.5, 0.5, ALU.mult, ALU.add)
                    V.tensor_scalar(w12[:, :, 1], th_g[:], -0.5, 0.5, ALU.mult, ALU.add).then_inc(w12_s, 1)
                    till(dve, topf_s, n[3])
                    V.tensor_tensor(oh[:], iota[:].unsqueeze(1).unsqueeze(1).to_broadcast([P, T, 2, E]),
                                    topf[:].unsqueeze(3).to_broadcast([P, T, 2, E]), ALU.is_equal).then_inc(oh_s, 1)
                if on[2]:
                    for pair in range(BLK):
                        till(dve, pv_ready[pair], n[2])
                    till(dve, thu_s, n[2])
                    till(dve, wo_ready, n[2] - 1)
                    V.scalar_tensor_tensor(gated[:], th_u[:, (off - 2) % 2], 1.0, AT_BANK[:], ALU.add, ALU.mult)\
                        .then_inc(gated_s, 1)
                if on[3]:
                    till(dve, oh_s, n[3])
                    till(dve, w12_s, n[3])
                    V.tensor_tensor(ohw[:], oh[:], w12[:].unsqueeze(3).to_broadcast([P, T, 2, E]), ALU.mult)\
                        .then_inc(ohw_s, 1)
                if on[1]:
                    norm_sums(2, n[1])
                if on[3]:
                    till(dve, ohw_s, n[3])
                    till(dve, wT_ready, n[3] - 1)
                    V.tensor_tensor(wt[:], ohw[:, :, 0], ohw[:, :, 1], ALU.add).then_inc(wt_s, 1)
            drive2(dve, step2)

        @block.gpsimd
        def _(pool):
            Q = nc.gpsimd
            pool.wait_ge(consts, 3)

            def step1(j, off, m):
                on, n = stages1(j, off, m)
                par = off % 2
                if on[1]:
                    till_alone(pool, nb1_s, n[1])
                    for k in POOL_TILES:
                        x_t, rstd, shift = group_tile(k, off, 1)
                        last = Q.tensor_scalar(x_t, x_t, rstd, shift, ALU.mult, ALU.add)
                    last.then_inc(xn1_pool, 1)
                if on[0]:
                    till(pool, ve1_s, n[0])
                    for done in (xn1_dve, xn1_act, xn1_pool, tab_s):
                        till(pool, done, n[0] - 2)
                    Q.tensor_tensor(ln1[:, par, :, 0, :], ve1[:, par].rearrange("p (r t) -> p r t", r=GR),
                                    neg_half[:].rearrange("p (r t) -> p r t", r=GR), ALU.pow).then_inc(rs1_s, 1)
            drive1(pool, step1)
            pool.wait_ge(rest_in, 16 * 5)
            pool.wait_ge(mt_s, T)
            pool.wait_ge(tab_s, GROUPS)

            mask_rows = maskT[:].rearrange("p s a t -> p (s a) t")

            def entry(table, row):
                return table[:, row, :] if isinstance(row, int) else table[:, bass.ds(row, 1), :].squeeze(1)

            def normalise(j, off, n):
                till(pool, x_in[off % 4], 16 * (j + off // 4 + 1))
                till_alone(pool, xn_s, n - 1)
                Q.tensor_copy(ln_row[:], entry(ln_table, n - 1)).then_inc(lnrow_s, 1)
                till(pool, lnrow_s, n)
                till_alone(pool, xt_ready, n - 2)
                for t in range(T):
                    last = Q.tensor_scalar(xn[:, off % 2, t], xin[:, off % 4, t], ln_row[:, t:t + 1],
                                           ln_row[:, T + t:T + t + 1], ALU.mult, ALU.add)
                last.then_inc(xn_s, 1)

            def residual(j, off, n):
                till(pool, x_in[off % 4], 16 * (j + off // 4 + 1))
                till_alone(pool, bom_s, n - 1)
                Q.tensor_copy(m_row[:], entry(mask_rows, n - 1)).then_inc(mrow_s, 1)
                till(pool, mrow_s, n)
                till_alone(pool, xb_s, n - 1)
                for t in range(T):
                    last = Q.tensor_scalar(bom[:, t], bo_rows[:], m_row[:, t:t + 1], 1.0, ALU.mult, ALU.mult)
                last.then_inc(bom_s, 1)
                till(pool, bom_s, n)
                till(pool, x1_s, n - 2)
                Q.tensor_tensor(xb[:, off % 2], xin[:, off % 4], bom[:], ALU.add).then_inc(xb_s, 1)

            def half_sum(buf, t, n):
                till(pool, yc_s[t], n)
                till(pool, ya_s[t], n)
                till(pool, yb_s[t], n)
                Q.tensor_tensor(Y[:, buf, t, 0:4 * D], Y[:, buf, t, 0:4 * D], Y[:, buf, t, 4 * D:8 * D],
                                ALU.add).then_inc(half_s[t], 1)

            def step2(j, off, i):
                on, n = stages2(j, off, i)
                if on[0]:
                    normalise(j, off, n[0])
                if on[2]:
                    residual(j, off - 2, n[2])
                if on[3]:
                    till(pool, ve2_s, n[3])
                    till(pool, tn_s, n[3] - 1)
                    Q.tensor_tensor(rstd2[:], ve2[:], neg_half[:, 0:T], ALU.pow).then_inc(rstd2_s, 1)
                    till(pool, x1_s, n[3])
                    till(pool, nmr_s, n[3])
                    till_alone(pool, tt_ready, n[3] - 1)
                    for t in range(T):
                        last = Q.tensor_scalar(tn[:, t], x1[:, t], rstd2[:, t:t + 1], nmr[:, t:t + 1],
                                               ALU.mult, ALU.add)
                    last.then_inc(tn_s, 1)
                if on[4]:
                    half_sum((off - 4) % 2, 0, n[4])
                if on[0]:
                    till(pool, xthi_s, n[0])
                    xt_used(pool, n[0] - 1)
                    Q.tensor_tensor(xt[1][:], xt_f[:], xt[0][:].bitcast(F32), ALU.subtract).then_inc(xtlo_s, 1)
                if on[4]:
                    half_sum((off - 4) % 2, 1, n[4])
                    for t in range(T):
                        till(pool, half_s[t], n[4])
                    yk = Y[:, (off - 4) % 2]
                    Q.tensor_tensor(yk[:, :, 0:2 * D], yk[:, :, 0:2 * D], yk[:, :, 2 * D:4 * D], ALU.add)\
                        .then_inc(quarter_s, 1)
                    till(pool, quarter_s, n[4])
                    till(pool, stored[(off - 4) % 2], 16 * (2 * j + (off - 4) // 2))
                    yk = Y[:, (off - 4) % 2]
                    Q.tensor_tensor(outb[:, (off - 4) % 2], yk[:, :, 0:D], yk[:, :, D:2 * D], ALU.add)\
                        .then_inc(ysum_s, 1)
                    till(pool, ysum_s, n[4])
                    till(pool, x1w_s, n[4])
                    Q.tensor_tensor(outb[:, (off - 4) % 2], outb[:, (off - 4) % 2], x1w[:], ALU.add).then_inc(out_s, 1)
            drive2(pool, step2)


_INS = ['x', 'L0_conv_mask', 'L0_conv_gamma', 'L0_conv_beta', 'L0_conv_Wq', 'L0_conv_Wk', 'L0_conv_Wv', 'L0_conv_Wb',
        'L0_conv_Wu', 'L0_conv_bu', 'L0_conv_Wo', 'L0_conv_bo', 'L0_ffn_router_w', 'L0_ffn_router_b',
        'L0_ffn_expert_w', 'L0_ffn_expert_b']


def kernel(**inputs):
    import numpy as _np
    import concourse.bacc as _bacc
    from concourse import mybir as _mybir
    from concourse.bass_utils import run_bass_kernel_spmd as _run

    nc = _bacc.Bacc("TRN2", target_bir_lowering=False, num_devices=1)
    given = {name: _np.ascontiguousarray(inputs[name]) for name in _INS}
    given["eye"] = _np.eye(128, dtype=_np.float32)
    given["iota8"] = _np.tile(_np.arange(8, dtype=_np.float32), (128, 1))
    arrays, args = {}, []
    for name, a in given.items():
        arrays[f"in_{name}_dram"] = a
        args.append(nc.dram_tensor(f"in_{name}_dram", a.shape, _mybir.dt.from_np(a.dtype), kind="ExternalInput").ap())
    args.append(nc.dram_tensor("out_0_dram", given["x"].shape, _mybir.dt.float32, kind="ExternalOutput").ap())
    metaformer_kernel(nc, *args)
    r = _run(nc, [arrays], core_ids=[0])
    return r.results[0]["out_0_dram"]
```
